# Optimizing a Trainium2 kernel written in Bass

```python
import numpy as np
import jax
import jax.numpy as jnp

def _softmax(x, axis=-1):
    return jax.nn.softmax(x, axis=axis)

def _gelu(x):
    return jax.nn.gelu(x, approximate=True)

def _silu(x):
    return jax.nn.silu(x)

def _sigmoid(x):
    return jax.nn.sigmoid(x)

def _layernorm(x, axis=-1, eps=1e-05):
    m = jnp.mean(x, axis=axis, keepdims=True)
    v = jnp.var(x, axis=axis, keepdims=True)
    return (x - m) / jnp.sqrt(v + eps)

def _scatter_add(tgt, idx, src, axis=0):
    return tgt.at[idx].add(src)

def _segment_sum(src, seg, n):
    return jax.ops.segment_sum(src, seg, n)
kernel_name = 'mk_seq_preln_d1_jaxref_r4_7e21e1'

def setup_inputs(seed: int=0):
    np.random.seed(seed)
    _w = jnp.asarray

    def _L0_attn_setup():
        import jax, jax.numpy as jnp
        import numpy as np
        EMBED_DIM = 256
        EXPAND_RATIO = 128
        B, N = (4, 512)

        def _rmsnorm(x, w, eps=1e-06):
            return x * jax.lax.rsqrt(jnp.mean(x * x, axis=-1, keepdims=True) + eps) * w

        def _gla_scan(q, k, v, g):
            b, n, h, d = q.shape
            qs, ks_, vs, gs = (jnp.moveaxis(t, 1, 0) for t in (q, k, v, g))
            S0 = jnp.zeros((b, h, d, d), dtype=q.dtype)

            def step(S, inp):
                q_t, k_t, v_t, g_t = inp
                S = jnp.exp(g_t)[..., :, None] * S + k_t[..., :, None] * v_t[..., None, :]
                o_t = jnp.einsum('bhk,bhkv->bhv', q_t, S)
                return (S, o_t)
            _, outs = jax.lax.scan(step, S0, (qs, ks_, vs, gs))
            return jnp.moveaxis(outs, 0, 1)
        key = jax.random.key(seed)
        ks = jax.random.split(key, 6)
        std = 0.02
        d = EMBED_DIM
        return {'x': jax.random.normal(ks[0], (B, N, d), dtype=jnp.float32), 'Wq': jax.random.normal(ks[1], (d, d), dtype=jnp.float32) * std, 'Wk': jax.random.normal(ks[2], (d, d), dtype=jnp.float32) * std, 'Wv': jax.random.normal(ks[3], (d, d), dtype=jnp.float32) * std, 'Wo': jax.random.normal(ks[4], (d, d), dtype=jnp.float32) * std, 'norm_w': jnp.ones((d,), dtype=jnp.float32)}
    _L0_attn_in = _L0_attn_setup()

    def _L0_ffn_setup():
        import jax, jax.numpy as jnp
        import numpy as np
        ALPHA = 1.702
        LIMIT = 9.0
        TOP_K = 2

        def swiglu(x):
            g, v = (x[..., 0::2], x[..., 1::2])
            g = jnp.clip(g, None, LIMIT)
            v = jnp.clip(v, -LIMIT, LIMIT)
            return g * jax.nn.sigmoid(ALPHA * g) * (v + 1)
        key = jax.random.key(seed)
        ks = jax.random.split(key, 6)
        B, L, D = (2, 512, 256)
        E, F = (8, 512)
        s_gate = 1.0 / np.sqrt(D)
        s1 = 1.0 / np.sqrt(D)
        s2 = 1.0 / np.sqrt(F)
        return {'x': jax.random.normal(ks[0], (B, L, D), dtype=jnp.float32), 'gate_w': jax.random.normal(ks[1], (D, E), dtype=jnp.float32) * s_gate, 'dense_1_w': jax.random.normal(ks[2], (E, 2 * F, D), dtype=jnp.float32) * s1, 'dense_1_b': jnp.zeros((E, 2 * F), dtype=jnp.float32), 'dense_2_w': jax.random.normal(ks[3], (E, D, F), dtype=jnp.float32) * s2, 'dense_2_b': jnp.zeros((E, D), dtype=jnp.float32)}
    _L0_ffn_in = _L0_ffn_setup()
    _d = {'L0_attn_x': _L0_attn_in['x'], 'L0_attn_Wq': _L0_attn_in['Wq'], 'L0_attn_Wk': _L0_attn_in['Wk'], 'L0_attn_Wv': _L0_attn_in['Wv'], 'L0_attn_Wo': _L0_attn_in['Wo'], 'L0_attn_norm_w': _L0_attn_in['norm_w'], 'L0_ffn_gate_w': _L0_ffn_in['gate_w'], 'L0_ffn_dense_1_w': _L0_ffn_in['dense_1_w'], 'L0_ffn_dense_1_b': _L0_ffn_in['dense_1_b'], 'L0_ffn_dense_2_w': _L0_ffn_in['dense_2_w'], 'L0_ffn_dense_2_b': _L0_ffn_in['dense_2_b']}
    _x0 = _d['L0_attn_x']
    _d['L0_attn_x'] = jax.random.normal(jax.random.fold_in(jax.random.key(seed), 1), (8, 512, 256), dtype=_x0.dtype)
    del _x0
    return _d

def reference(L0_attn_x, L0_attn_Wq, L0_attn_Wk, L0_attn_Wv, L0_attn_Wo, L0_attn_norm_w, L0_ffn_gate_w, L0_ffn_dense_1_w, L0_ffn_dense_1_b, L0_ffn_dense_2_w, L0_ffn_dense_2_b):

    def _L0_attn_ref(x, Wq, Wk, Wv, Wo, norm_w):
        import jax, jax.numpy as jnp
        import numpy as np
        EMBED_DIM = 256
        EXPAND_RATIO = 128
        B, N = (4, 512)

        def _rmsnorm(x, w, eps=1e-06):
            return x * jax.lax.rsqrt(jnp.mean(x * x, axis=-1, keepdims=True) + eps) * w

        def _gla_scan(q, k, v, g):
            b, n, h, d = q.shape
            qs, ks_, vs, gs = (jnp.moveaxis(t, 1, 0) for t in (q, k, v, g))
            S0 = jnp.zeros((b, h, d, d), dtype=q.dtype)

            def step(S, inp):
                q_t, k_t, v_t, g_t = inp
                S = jnp.exp(g_t)[..., :, None] * S + k_t[..., :, None] * v_t[..., None, :]
                o_t = jnp.einsum('bhk,bhkv->bhv', q_t, S)
                return (S, o_t)
            _, outs = jax.lax.scan(step, S0, (qs, ks_, vs, gs))
            return jnp.moveaxis(outs, 0, 1)
        b, n, D = x.shape
        hd = EXPAND_RATIO
        h = D // hd
        q = jax.nn.silu(x @ Wq.T)
        f = jax.nn.sigmoid(x @ Wk.T)
        log_f = jax.nn.log_sigmoid(f)
        k = 1.0 - f
        v = x @ Wv.T

        def split_heads(t):
            return t.reshape(b, n, h, hd)
        out = _gla_scan(split_heads(q), split_heads(k), split_heads(v), split_heads(log_f))
        out = out.reshape(b, n, D)
        out = _rmsnorm(out, norm_w)
        return out @ Wo.T

    def _L0_ffn_ref(x, gate_w, dense_1_w, dense_1_b, dense_2_w, dense_2_b):
        import jax, jax.numpy as jnp
        import numpy as np
        ALPHA = 1.702
        LIMIT = 9.0
        TOP_K = 2

        def swiglu(x):
            g, v = (x[..., 0::2], x[..., 1::2])
            g = jnp.clip(g, None, LIMIT)
            v = jnp.clip(v, -LIMIT, LIMIT)
            return g * jax.nn.sigmoid(ALPHA * g) * (v + 1)
        B, L, D = x.shape
        xf = x.reshape(B * L, D)
        gate = xf @ gate_w
        weights, sel = jax.lax.top_k(gate, k=TOP_K)
        weights = jax.nn.softmax(weights, axis=-1)
        h = jnp.einsum('ecd,td->tec', dense_1_w, xf) + dense_1_b[None]
        h = swiglu(h)
        y = jnp.einsum('edf,tef->ted', dense_2_w, h) + dense_2_b[None]
        y_sel = jnp.take_along_axis(y, sel[:, :, None], axis=1)
        out = jnp.einsum('tkd,tk->td', y_sel, weights)
        return out.reshape(B, L, D)
    x = L0_attn_x
    x = x + _L0_attn_ref(_layernorm(x, axis=-1), L0_attn_Wq, L0_attn_Wk, L0_attn_Wv, L0_attn_Wo, L0_attn_norm_w)
    x = x + _L0_ffn_ref(_layernorm(x, axis=-1), L0_ffn_gate_w, L0_ffn_dense_1_w, L0_ffn_dense_1_b, L0_ffn_dense_2_w, L0_ffn_dense_2_b)
    return x

_drawn_inputs = setup_inputs


def setup_inputs(seed=0):
    import zlib

    import numpy as np

    out = dict(_drawn_inputs(seed))
    spreads = {'L0_attn_norm_w': (1.0, 0.2),
     'L0_ffn_dense_1_b': (0.0, 0.1),
     'L0_ffn_dense_2_b': (0.0, 0.1)}
    factors = {}
    for name, (base, spread) in spreads.items():
        noise = np.random.default_rng([zlib.crc32(name.encode()), seed]).standard_normal(out[name].shape)
        drawn = base * np.exp(spread * noise) if base else spread * noise
        out[name] = jnp.asarray(drawn.astype(out[name].dtype))
    for name, factor in factors.items():
        out[name] = (out[name] * factor).astype(out[name].dtype)
    return out
```

```python
import math
from contextlib import ExitStack

import concourse.bass as bass
from concourse import mybir

ALU = mybir.AluOpType
ACT = mybir.ActivationFunctionType
AX = mybir.AxisListType.X
F32 = mybir.dt.float32
F16 = mybir.dt.float16
I32 = mybir.dt.int32

P = 128
NSEQ, L, D = 8, 512, 256
T = NSEQ * L
C = L // P
KD = D // P
NH = KD
HALF = P // 2
E, FF = 8, 512
FJ = FF // P
RT = 256
SR = RT // P
REGION = T + RT
SPARE = E * REGION
NT = 2 * T // RT + E - 1
ROW = 2 * D + 8
WORDS = ROW // 2

SX = 2.0 ** 11
SW = 2.0 ** 8
SH = 2.0 ** 8
ALPHA, LIMIT = 1.702, 9.0
SILU_MAX = ALPHA * LIMIT / (1 + math.exp(-ALPHA * LIMIT))
EPS_LN, EPS_RMS = 1e-5, 1e-6
WCH = 1024
W1COLS, W2COLS = E * KD * 2 * FF, E * FJ * D
NCH = (W1COLS + W2COLS) // WCH
CPS = NCH // NSEQ
SETUP, ROUTE_A, ROUTE_B, PLAN, WSTEPS = 12, 13, 10, 18, 4

CF = {}
_at = 0
for _name, _n in (("ident", P), ("mask", P), ("base", E), ("tie", E), ("eidx", E), ("tile", NT), ("tile_row", NT),
                  ("half", C), ("ones", E), ("low", 1), ("tok", T // P)):
    CF[_name] = (_at, _at + _n)
    _at += _n
CFN = _at


class Seq:

    def __init__(self, j, c):
        self.j, self.c = j, c
        self.n = 2 * j + c
        self.par = c % 2
        self.half = j + c // 2

    def upto(self, per, count=None):
        return self.n * per + (per if count is None else count)

    def upto_half(self, per):
        return self.half * per + per


def build_kernel(nc, x, wqkv, wo, norm_w, gate_w, we, b1, b2, cf, ch, pad, out):
    rows_dram = nc.dram_tensor("dispatched_rows", (SPARE + REGION, WORDS), I32).ap()

    with ExitStack() as ctx:
        def sb(name, shape, dt=F32):
            return ctx.enter_context(nc.sbuf_tensor(name, shape, dt))

        def sem(name):
            return ctx.enter_context(nc.semaphore(name))

        wes = sb("wes", [P, 2, W1COLS + W2COLS], F16)
        wst = sb("wst", [P, 2, WCH])
        wp = sb("wp", [P, 2, 3, KD, D], F16)
        wos = sb("wos", [P, NH, D])
        nws = sb("nws", [P, NH])
        gws = sb("gws", [P, KD, E])
        b1s = sb("b1s", [P, E * 2 * FJ])
        b2s = sb("b2s", [2, E * D], F16)
        ones2 = sb("ones2", [2, P], F16)
        cfs = sb("cfs", [P, CFN])
        chs = sb("chs", [P, 3 * P], F16)
        xs = sb("xs", [P, 2, C, D])
        xr = sb("xr", [P, C, D])
        xhl = sb("xhl", [P, 2, C, D], F16)
        xT = sb("xT", [P, 2, KD, L], F16)
        ff = sb("ff", [P, NH * L])
        kk = sb("kk", [P, NH, L])
        qq = sb("qq", [P, NH, L])
        resets = sb("resets", [P, NH * L])
        qt = sb("qt", [P, 2, NH, L])
        vv = sb("vv", [P, 2, C, D])
        at = sb("at", [P, NH, C, P])
        kTs = sb("kTs", [P, NH, C - 1, P])
        sm = sb("sm", [P, C - 1, NH, P])
        smt = sb("smt", [P, NH, P])
        ots = sb("ots", [P, NH, L])
        xn2 = sb("xn2", [P, C, D])
        x2T = sb("x2T", [P, KD, L])
        rows = sb("rows", [P, 2, C, ROW], F16)
        st = sb("st", [P, C, 6])
        st2 = sb("st2", [P, C, 6])
        mv1 = sb("mv1", [P, C, 2])
        mv2 = sb("mv2", [P, C, 2])
        pw = sb("pw", [P, 4, C])
        rs1 = sb("rs1", [P, C])
        rms = sb("rms", [P, C])
        rs2 = sb("rs2", [P, C])
        ssv = sb("ssv", [P, C])
        dmid = sb("dmid", [P, NH * C])
        dend = sb("dend", [P, NH * C])
        rmid = sb("rmid", [P, NH * C])
        gg = sb("gg", [P, NH, C - 1])
        rt = sb("rt", [P, 6, C, E])
        rc = sb("rc", [P, 8, C])
        msel = sb("msel", [P, C, E], F16)
        wsig = sb("wsig", [P, 2, C])
        cnt = sb("cnt", [P, E])
        dest = sb("dest", [P, 2, 2, C], I32)
        plan = sb("plan", [P, 4, E])
        plani = sb("plani", [P, 3, E], I32)
        pt = sb("pt", [P, 4, NT])
        roff = sb("roff", [P, NT], I32)
        etab = sb("etab", [P, NT], I32)
        pads = sb("pads", [P, SR, WORDS], I32)
        meta = sb("meta", [P, 2, SR, 3])
        token = sb("token", [P, 2, SR], I32)
        wrow = sb("wrow", [P, 2, 2, SR])

        ps = ctx.enter_context(nc.psum_tensor("ps", [P, 8, 512], F32))

        def bank(i):
            return ps[:, i, :]

        def bank16(i):
            return ps[:, i, :].bitcast(F16)

        def const(name):
            a, b = CF[name]
            return cfs[:, a:b]

        identh, upper, ones16 = chs[:, 0:P], chs[:, P:2 * P], chs[:, 2 * P:3 * P]
        ident = const("ident")

        names = """x_in0 x_in1 xr_in x2_out small_in wq_in wo_in const_in st_in0 st_in1 pads_in pad_out zero_out
            setup split_high split_low we_scaled we_high we_low
            ln1_stats ln1_mv ln1_var rstd1 xn_ready xh_ready xl_ready t1_done xT_ready kp_done qp_done vp_done
            sig_k dec_ready sig_q v_ready scan_prep scan_done mid_done rmid_done e_done q_done qt_ready re_done kt_ready
            a_done at_ready kt_done kts_ready kv_done sm_ready ot_done ots_ready sq_ready ss_done ssv_ready rms_ready
            y_done x2_ready ln2_stats ln2_mv ln2_var rstd2 xn2_ready rowhi_ready rowlo_ready x2t_done x2T_ready lg_done
            route_a wsig_ready rk_done route_b tok_ready disp0 disp1 plan_done
            xg_in0 xg_in1 tx_done xtc_ready g1_done sv_ready h_ready g2_done y_ready meta_ready w_ready added held""".split()
        S = {n: sem(n) for n in names}
        x_in, disp, st_in, xg_in = ([S[f"{n}{i}"] for i in range(2)] for n in ("x_in", "disp", "st_in", "xg_in"))

        rows32 = rows[:].bitcast(F32)
        rows_i = rows[:].bitcast(I32)
        wq_stage = qt[:].rearrange("p a h l -> p (a h l)")[:, 0:3 * KD * D]

        def flat(t):
            names = " ".join("abcde"[:len(t.shape) - 1])
            return t[:].rearrange(f"p {names} -> p ({names})") if len(t.shape) > 2 else t[:]

        def xTm(i):
            return flat(xT)[:, i.par * 4 * RT:(i.par + 1) * 4 * RT].rearrange("p (q t) -> p q t", t=RT)

        def silu_of(i):
            return flat((kk, qq)[i.par]).rearrange("p (q t) -> p q t", t=RT)

        def value_of(i):
            return flat((ff, at)[i.par]).rearrange("p (q t) -> p q t", t=RT)

        def hhl(i):
            return flat((ots, xn2)[i.par]).bitcast(F16).rearrange("p (a q t) -> p a q t", a=2, t=RT)

        def y_of(i):
            return flat(x2T)[:, i.par * SR * D:(i.par + 1) * SR * D].rearrange("p (s d) -> p s d", d=D)

        block = ctx.enter_context(nc.Block())

        x_v = x.rearrange("(s p) d -> p s d", p=P)
        out_v = out.rearrange("(s p) d -> p s d", p=P)

        def wait(eng, name, value):
            if isinstance(value, int) and value <= 0:
                return
            eng.wait_ge(S[name] if isinstance(name, str) else name, value)

        def wait_apart(eng, *waits):
            for name, v in waits:
                wait(eng, name, v)
                if not isinstance(v, int):
                    eng.sem_inc(S["held"], 1)

        def pipelined(eng, first, last, one):
            assert (last - first + 1) % 2 == 0
            with eng.Fori(0, (last - first + 1) // 2) as j:
                for u in range(2):
                    one(j, first + u)

        @block.sync
        def _(sp):
            sp.dma_start(cfs[:], cf).then_inc(S["const_in"], 16)
            sp.dma_start(xs[:, 0], x_v[:, 0:C]).then_inc(x_in[0], 16)
            sp.dma_start(chs[:], ch).then_inc(S["const_in"], 16)
            sp.dma_start(qt[:].rearrange("p a h l -> p (a h l)")[:, 0:3 * KD * D], wqkv).then_inc(S["wq_in"], 16)
            sp.dma_start(xs[:, 1], x_v[:, C:2 * C]).then_inc(x_in[1], 16)
            sp.dma_start(wos[:], wo).then_inc(S["wo_in"], 16)
            sp.dma_start(nws[:], norm_w).then_inc(S["wo_in"], 16)
            sp.dma_start(gws[:], gate_w).then_inc(S["small_in"], 16)
            sp.dma_start(b1s[:], b1).then_inc(S["small_in"], 16)
            for p in range(2):
                sp.dma_start(vv[p:p + 1].rearrange("p a c d -> p (a c d)"), b2).then_inc(S["small_in"], 16)
            sp.dma_start(pads[:], pad).then_inc(S["pads_in"], 16)
            sp.dma_start(xr[:], x_v[:, 0:C]).then_inc(S["xr_in"], 16)
            sp.wait_ge(S["pads_in"], 16)
            sp.dma_start(rows_dram[SPARE:SPARE + RT, :].rearrange("(s p) n -> p s n", p=P), pads[:]).then_inc(S["pad_out"], 16)
            sp.wait_ge(S["setup"], 1)
            sp.dma_start(out_v[:, T // P:T // P + SR, :], resets[:, 0:SR * D].rearrange("p (s d) -> p s d", d=D)).then_inc(S["zero_out"], 16)

            def weights_in(m, slot):
                wait_apart(sp, ("we_low", m - 1))
                sp.dma_start(wst[:, slot], we[:, bass.ds(m * WCH, WCH)]).then_inc(st_in[slot], 16)

            weights_in(0, 0)
            weights_in(1, 1)

            def one(j, c, load=True, keep=True):
                b = Seq(j, c)
                if load:
                    a = Seq(j, c + 2)
                    wait_apart(sp, ("xl_ready", b.upto(1)),
                                   ("ss_done", b.upto(1, 0)))
                    sp.dma_start(xs[:, a.par], x_v[:, bass.ds(a.n * C, C)]).then_inc(x_in[a.par], 16)
                for q in range(CPS if keep else CPS - 2):
                    weights_in(b.n * CPS + 2 + q, (CPS * c + q) % 2)
                wait_apart(sp, ("x2_ready", b.upto(C)))
                sp.dma_start(out_v[:, bass.ds(b.n * C, C)], xr[:]).then_inc(S["x2_out"], 16)
                if keep:
                    wait_apart(sp, ("x2_out", b.upto(16)), ("xn2_ready", b.upto(C)))
                    a = Seq(j, c + 1)
                    sp.dma_start(xr[:], x_v[:, bass.ds(a.n * C, C)]).then_inc(S["xr_in"], 16)

            one(0, 0)
            pipelined(sp, 1, 4, one)
            one(0, 5)
            one(0, 6, load=False)
            one(0, 7, load=False, keep=False)
            sp.wait_ge(S["plan_done"], PLAN)
            for e in range(E):
                row = sp.value_load(plani[0:1, 2, e:e + 1], min_val=0, max_val=SPARE - RT)
                sp.dma_start(rows_dram[bass.ds(row, RT), :].rearrange("(s p) n -> p s n", p=P), pads[:]).then_inc(S["pad_out"], 16)
            sp.wait_ge(S["pad_out"], 16 * (E + 1))
            for i in range(2):
                sp.wait_ge(disp[i], 16 * 2 * C * NSEQ // 2)

            def tile_in(j, c):
                i = Seq(j, c)
                wait_apart(sp, ("tx_done", i.upto(1, -1)),
                               ("meta_ready", i.upto(2, -2)))
                row = sp.value_load(roff[0:1, bass.ds(i.n, 1)], min_val=0, max_val=SPARE)
                sp.dma_start(rows_i[:, i.par, 0:SR], rows_dram[bass.ds(row, RT), :].rearrange("(s p) n -> p s n", p=P)).then_inc(xg_in[i.par], 16)

            for c in range(3):
                tile_in(0, c)
            pipelined(sp, 3, NT - 1, tile_in)
            sp.wait_ge(S["x2_out"], 16 * NSEQ)
            sp.wait_ge(S["zero_out"], 16)
            sp.wait_ge(S["added"], 32 * NT)


        @block.tensor
        def _(pe):
            def chunk(c):
                return slice(c * P, (c + 1) * P)

            def transposed_x(b):
                wait(pe, "y_done", b.upto(2, -2))
                wait(pe, "x2_ready", b.upto(C, -C))
                for part in range(2):
                    wait(pe, ("xh_ready", "xl_ready")[part], b.upto(1))
                    for k in range(KD):
                        for c in range(C):
                            mm = pe.transpose(bank16(part)[:, k * L + c * P:k * L + (c + 1) * P],
                                              xhl[:, part, c, k * P:(k + 1) * P], identh)
                    mm.then_inc(S["t1_done"], 1)

            def three(o, lhs, rhs):
                terms = [(k, a, c) for k in range(KD) for a, c in ((0, 0), (0, 1), (1, 0))]
                for n, (k, a, c) in enumerate(terms):
                    mm = pe.matmul(o, lhs(a, k), rhs(c, k), start=n == 0, stop=n == len(terms) - 1)
                return mm

            def project_heads(b, which, name):
                for h in range(NH):
                    if which == 1:
                        wait(pe, "v_ready", b.upto(2, h - 1))
                        if h == 0:
                            wait(pe, "xT_ready", b.upto(2))
                    else:
                        wait(pe, "sig_k", b.upto(2 * NH, 2 * h + 2))
                    three(bank(2 + h), lambda a, k: wp[:, a, which, k, h * P:(h + 1) * P],
                          lambda a, k: xT[:, a, k, :]).then_inc(S[name], 1)

            def project_v(b):
                for pair in range(2):
                    wait(pe, "q_done", b.upto(NH, pair + 1))
                    for c in range(2 * pair, 2 * pair + 2):
                        mm = three(bank(2 + pair)[:, c % 2 * D:(c % 2 + 1) * D],
                                   lambda a, k: xT[:, a, k, chunk(c)], lambda a, k: wp[:, a, 2, k, :])
                    mm.then_inc(S["vp_done"], 1)

            def scores(b):
                wait(pe, "kt_ready", b.upto(1))
                wait(pe, "qt_ready", b.upto(1))
                wait(pe, "ssv_ready", b.upto(1, 0))
                wait(pe, "route_b", b.upto(ROUTE_B, 2 - 2 * ROUTE_B))
                for h in range(NH):
                    for c in range(C):
                        mm = pe.matmul(bank(4 + h)[:, chunk(c)], kk[:, h, chunk(c)], qt[:, b.par, h, chunk(c)],
                                       start=True, stop=True)
                    mm.then_inc(S["a_done"], 1)

            def keys(b):
                for h in range(NH):
                    wait(pe, "sq_ready", b.upto(NH, h + 1 - NH))
                    for c in range(C - 1):
                        mm = pe.transpose(bank(6 + h)[:, chunk(c)], kk[:, h, chunk(c)], ident)
                    mm.then_inc(S["kt_done"], 1)

            def states(b):
                wait(pe, "at_ready", b.upto(2 * NH))
                wait(pe, "kts_ready", b.upto(NH))
                wait(pe, "v_ready", b.upto(2))
                for h in range(NH):
                    for c in range(C - 1):
                        mm = pe.matmul(bank(4 + h)[:, chunk(c)], kTs[:, h, c, :], vv[:, b.par, c, h * P:(h + 1) * P],
                                       start=True, stop=True)
                mm.then_inc(S["kv_done"], 1)

            def outputs(b):
                wait(pe, "sm_ready", b.upto(5))
                for h in range(NH):
                    for c in range(C):
                        mm = pe.matmul(bank(6 + h)[:, chunk(c)], vv[:, b.par, c, h * P:(h + 1) * P], at[:, h, c, :],
                                       start=True, stop=c == 0)
                        if c:
                            mm = pe.matmul(bank(6 + h)[:, chunk(c)], sm[:, c - 1, h, :], qt[:, b.par, h, chunk(c)],
                                           start=False, stop=True)
                    mm.then_inc(S["ot_done"], 1)

            def squares(b):
                wait(pe, "sq_ready", b.upto(NH))
                for c in range(C):
                    for h in range(NH):
                        mm = pe.matmul(bank(4)[:, c:c + 1], xs[:, 1 - b.par].rearrange("p c d -> p (c d)")[:, h * L + c * P:h * L + (c + 1) * P],
                                       const("ones")[:, 0:1], start=h == 0, stop=h == NH - 1)
                mm.then_inc(S["ss_done"], 1)

            def mixed(b):
                wait(pe, "x2T_ready", b.upto(KD, 0))
                for c in range(C):
                    for h in range(NH):
                        mm = pe.matmul(bank(c // 2)[:, c % 2 * D:(c % 2 + 1) * D], ots[:, h, chunk(c)], wos[:, h, :],
                                       start=h == 0, stop=h == NH - 1)
                    if c % 2:
                        mm.then_inc(S["y_done"], 1)

            def transposed_x2(b, last=False):
                wait(pe, "xn2_ready", b.upto(C))
                if not last:
                    wait(pe, "xT_ready", b.upto(2, 6))
                for k in range(KD):
                    for c in range(C):
                        mm = pe.transpose(bank(k)[:, chunk(c)], xn2[:, c, k * P:(k + 1) * P], ident)
                    mm.then_inc(S["x2t_done"], 1)

            def gates(b, last=False):
                wait(pe, "x2T_ready", b.upto(KD))
                if not last:
                    wait(pe, "sm_ready", b.upto(5, 10))
                for c in range(C):
                    for k in range(KD):
                        mm = pe.matmul(bank(5)[:, c * E:(c + 1) * E], x2T[:, k, chunk(c)], gws[:, k, :],
                                       start=k == 0, stop=k == KD - 1)
                mm.then_inc(S["lg_done"], 1)

            def ranks(b):
                wait(pe, "route_a", b.upto(ROUTE_A))
                for c in range(C):
                    for d in range(c + 1):
                        mm = pe.matmul(bank(5)[:, 64 + c * E:64 + (c + 1) * E], upper if d == c else ones16, msel[:, d, :],
                                       start=d == 0, stop=d == c)
                for d in range(C):
                    mm = pe.matmul(bank(5)[:, 128:128 + E], ones16, msel[:, d, :], start=d == 0, stop=d == C - 1)
                mm.then_inc(S["rk_done"], 1)

            def one(j, c, f=True, r=True, b_=True):
                a, b, z = Seq(j, c + 1), Seq(j, c), Seq(j, c - 1)
                if b_:
                    scores(b)
                    keys(b)
                    states(b)
                if f:
                    transposed_x(a)
                if r:
                    transposed_x2(z, last=not f)
                if f:
                    project_heads(a, 1, "kp_done")
                if r:
                    gates(z, last=not b_)
                if f:
                    project_heads(a, 0, "qp_done")
                    project_v(a)
                if r:
                    ranks(z)
                if b_:
                    outputs(b)
                    squares(b)
                    mixed(b)

            pe.wait_ge(S["const_in"], 32)
            pe.wait_ge(S["small_in"], 64)
            pe.wait_ge(S["split_low"], 1)
            pe.wait_ge(S["setup"], SETUP)
            one(0, -1, r=False, b_=False)
            one(0, 0, r=False)
            one(0, 1)
            pipelined(pe, 2, 5, one)
            one(0, 6)
            one(0, 7, f=False)
            one(0, 8, f=False, b_=False)

            def tile_transposed(i):
                wait(pe, xg_in[i.par], i.upto_half(16))
                wait(pe, "xtc_ready", i.upto(1, -1))
                for part in range(2):
                    for k in range(KD):
                        for s in range(SR):
                            mm = pe.transpose(bank16(4 + i.par)[:, (2 * part + k) * RT + s * P:(2 * part + k) * RT + (s + 1) * P],
                                              rows[:, i.par, s, part * D + k * P:part * D + (k + 1) * P], identh)
                mm.then_inc(S["tx_done"], 1)

            def up(i, e):
                pe.wait_ge(S["xtc_ready"], i.upto(1))
                for j in range(FJ):
                    wait(pe, "sv_ready", i.upto(2 * FJ, 2 * j + 2 - 2 * FJ))
                    for g in range(2):
                        terms = [(k, a, c) for k in range(KD) for a, c in ((0, 0), (0, 1), (1, 0))]
                        for n, (k, a, c) in enumerate(terms):
                            lhs = wes[:, a, bass.ds(e * (KD * 2 * FF) + (k * 2 * FF + g * FF + j * P), P)]
                            mm = pe.matmul(bank(j)[:, g * RT:(g + 1) * RT], lhs, xTm(i)[:, 2 * c + k, :],
                                           start=n == 0, stop=n == len(terms) - 1)
                    mm.then_inc(S["g1_done"], 1)

            def down(i, e):
                pe.wait_ge(S["h_ready"], i.upto(4))
                wait(pe, "y_ready", i.upto(SR, -SR))
                for s in range(SR):
                    o = bank(6 + i.par)[:, s * D:(s + 1) * D]
                    pe.matmul(o, ones2[0:2, :], b2s[0:2, bass.ds(e * D, D)], start=True, stop=False)
                    for j in range(FJ):
                        for a, c in ((0, 0), (1, 0), (0, 1)):
                            rhs = wes[:, c, bass.ds(e * (FJ * D) + (W1COLS + j * D), D)]
                            mm = pe.matmul(o, hhl(i)[:, a, j, s * P:(s + 1) * P], rhs, start=False, stop=j == FJ - 1 and (a, c) == (0, 1))
                mm.then_inc(S["g2_done"], 1)

            def tile(j, c, t=True, u=True, d=True):
                i = Seq(j, c)
                if t:
                    tile_transposed(Seq(j, c + 1))
                if u:
                    up(i, pe.value_load(etab[0:1, bass.ds(i.n, 1)], min_val=0, max_val=E - 1))
                if d:
                    z = Seq(j, c - 1)
                    down(z, pe.value_load(etab[0:1, bass.ds(z.n, 1)], min_val=0, max_val=E - 1))

            tile(0, -1, u=False, d=False)
            tile(0, 0, d=False)
            for c in range(1, 4):
                tile(0, c)
            pipelined(pe, 4, NT - 2, tile)
            tile(0, NT - 1, t=False)
            tile(0, NT, t=False, u=False)

        @block.scalar
        def _(act):
            act.wait_ge(S["wq_in"], 16)
            act.activation(wq_stage, wq_stage, ACT.Copy, scale=SW).then_inc(S["split_high"], 1)
            act.wait_ge(S["split_high"], 1)
            act.activation(wp[:, 0].rearrange("p q k d -> p (q k d)"), wq_stage, ACT.Copy).then_inc(S["split_high"], 1)

            def split_weights(b, q, slot):
                m = b.n * CPS + q
                act.wait_ge(st_in[slot], (CPS * b.j + (CPS * b.c + q) // 2) * 16 + 16)
                act.activation(wst[:, slot], wst[:, slot], ACT.Copy, scale=SW).then_inc(S["we_scaled"], 1)
                act.wait_ge(S["we_scaled"], m + 1)
                act.activation(wes[:, 0, bass.ds(m * WCH, WCH)], wst[:, slot], ACT.Copy).then_inc(S["we_high"], 1)

            def one(j, c, f=True, r=True, b_=True):
                a, b, z = Seq(j, c + 1), Seq(j, c), Seq(j, c - 1)
                slot = lambda q: (CPS * c + q) % 2
                if b_:
                    for h in range(NH):
                        wait(act, "kt_done", b.upto(NH, h + 1))
                        act.activation(kTs[:, h], bank(6 + h)[:, 0:(C - 1) * P].rearrange("p (c t) -> p c t", t=P),
                                       ACT.Copy).then_inc(S["kts_ready"], 1)
                if f:
                    wait(act, "xn_ready", a.upto(C))
                    wait(act, "t1_done", a.upto(2, -1))
                    act.activation(xhl[:, 0], xs[:, a.par], ACT.Copy).then_inc(S["xh_ready"], 1)
                if b_:
                    split_weights(b, 0, slot(0))
                if f:
                    for part in range(2):
                        wait(act, "t1_done", a.upto(2, part + 1))
                        wait(act, "vp_done", a.upto(2, 0))
                        act.activation(xT[:, part], bank16(part).rearrange("p (k t) -> p k t", t=L), ACT.Copy)\
                            .then_inc(S["xT_ready"], 1)
                if b_:
                    split_weights(b, 1, slot(1))
                if r:
                    for k in range(KD):
                        act.wait_ge(S["x2t_done"], z.upto(KD, k + 1))
                        wait(act, "lg_done", z.upto(1, 0))
                        act.activation(x2T[:, k], bank(k), ACT.Copy).then_inc(S["x2T_ready"], 1)
                if f:
                    for h in range(NH):
                        act.wait_ge(S["kp_done"], a.upto(NH, h + 1))
                        if h == 0:
                            wait(act, "kt_ready", a.upto(1, 0))
                        act.activation(ff[:, h * L:(h + 1) * L], bank(2 + h), ACT.Sigmoid, scale=1 / (SX * SW)).then_inc(S["sig_k"], 1)
                        wait(act, "kt_done", a.upto(NH, 0))
                        act.activation(kk[:, h], bank(2 + h), ACT.Sigmoid, scale=-1 / (SX * SW)).then_inc(S["sig_k"], 1)
                    act.wait_ge(S["sig_k"], a.upto(2 * NH))
                    act.activation(ff[:], ff[:], ACT.Sigmoid).then_inc(S["dec_ready"], 1)
                if b_:
                    split_weights(b, 2, slot(2))
                if r:
                    act.wait_ge(S["route_a"], z.upto(ROUTE_A))
                    for n, sign in enumerate((1, -1)):
                        act.activation(wsig[:, n], rc[:, 6], ACT.Sigmoid, scale=sign / SX).then_inc(S["wsig_ready"], 1)
                if f:
                    for h in range(NH):
                        act.wait_ge(S["qp_done"], a.upto(NH, h + 1))
                        wait(act, "qt_ready", a.upto(1, 0))
                        act.activation(qq[:, h], bank(2 + h), ACT.Sigmoid, scale=1 / (SX * SW)).then_inc(S["sig_q"], 1)
                    for pair in range(2):
                        act.wait_ge(S["vp_done"], a.upto(2, pair + 1))
                        act.activation(vv[:, a.par, 2 * pair:2 * pair + 2].rearrange("p c d -> p (c d)"), bank(2 + pair), ACT.Copy,
                                       scale=1 / (SX * SW)).then_inc(S["v_ready"], 1)
                if b_:
                    sq = xs[:, 1 - b.par].rearrange("p c d -> p (c d)")
                    for h in range(NH):
                        act.wait_ge(S["ot_done"], b.upto(NH, h + 1))
                        wait(act, "y_done", b.upto(2, 0))
                        act.activation(ots[:, h], bank(6 + h), ACT.Copy).then_inc(S["ots_ready"], 1)
                        act.activation(sq[:, h * L:(h + 1) * L], bank(6 + h), ACT.Square).then_inc(S["sq_ready"], 1)
                    act.wait_ge(S["xn2_ready"], b.upto(C))
                    wait(act, disp[b.par], b.half * (2 * C * 16))
                    act.activation(rows[:, b.par, :, 0:D], xn2[:], ACT.Copy).then_inc(S["rowhi_ready"], 1)

            act.wait_ge(S["setup"], SETUP)
            one(0, -1, r=False, b_=False)
            one(0, 0, r=False)
            one(0, 1)
            one(0, 2)
            pipelined(act, 3, 6, one)
            one(0, 7, f=False)
            one(0, 8, f=False, b_=False)

            def tile(j, c, t=True, u=True):
                i = Seq(j, c)
                if t:
                    a = Seq(j, c + 1)
                    act.wait_ge(S["tx_done"], a.upto(1))
                    wait(act, "g1_done", a.upto(FJ, -FJ))
                    act.activation(xTm(a), bank16(4 + a.par).rearrange("p (q t) -> p q t", t=RT), ACT.Copy).then_inc(S["xtc_ready"], 1)
                if u:
                    e = act.value_load(etab[0:1, bass.ds(i.n, 1)], min_val=0, max_val=E - 1)
                    wait(act, "h_ready", i.upto(4, -4))
                    for q in range(FJ):
                        act.wait_ge(S["g1_done"], i.upto(FJ, q + 1))
                        act.activation(silu_of(i)[:, q, :], bank(q)[:, 0:RT], ACT.Silu, bias=b1s[:, bass.ds(e * 2 * FJ + q, 1)],
                                       scale=ALPHA / (SX * SW)).then_inc(S["sv_ready"], 1)
                        act.activation(value_of(i)[:, q, :], bank(q)[:, RT:2 * RT], ACT.Identity,
                                       bias=b1s[:, bass.ds(e * 2 * FJ + (FJ + q), 1)],
                                       scale=SH / (ALPHA * SX * SW)).then_inc(S["sv_ready"], 1)

            tile(0, -1, u=False)
            tile(0, 0)
            tile(0, 1)
            pipelined(act, 2, NT - 2, tile)
            tile(0, NT - 1, t=False)

        @block.vector
        def _(dve):
            def row_stats(b, src, st_, mv_, stats_sem, mv_sem):
                for c in range(C):
                    dve.bn_stats(st_[:, c, :], src[:, c, :]).then_inc(S[stats_sem], 1)
                wait_apart(dve, (S[stats_sem], b.upto(C)))
                for c in range(C):
                    dve.bn_aggr(mv_[:, c, :], st_[:, c, :]).then_inc(S[mv_sem], 1)

            def stats1(a):
                dve.wait_ge(x_in[a.par], a.upto_half(16))
                row_stats(a, xs[:, a.par], st, mv1, "ln1_stats", "ln1_mv")

            def normalise1(a):
                dve.wait_ge(S["rstd1"], a.upto(1))
                for c in range(C):
                    dve.tensor_scalar(xs[:, a.par, c], xs[:, a.par, c], mv1[:, c, 0:1], rs1[:, c:c + 1], ALU.subtract, ALU.mult)\
                        .then_inc(S["xn_ready"], 1)

            def low1(a):
                dve.wait_ge(S["xh_ready"], a.upto(1))
                wait(dve, "t1_done", a.upto(2, 0))
                dve.tensor_tensor(xhl[:, 1], xs[:, a.par], xhl[:, 0], ALU.subtract).then_inc(S["xl_ready"], 1)

            def decays(a):
                d = ff[:].rearrange("p (g s t) -> p g s t", s=2, t=HALF)
                starts = ff[:].rearrange("p (g t) -> p g t", t=HALF)[:, :, 0]
                dve.wait_ge(S["dec_ready"], a.upto(1))
                dve.tensor_copy(resets[:].rearrange("p (g t) -> p g t", t=HALF)[:, :, 0], starts).then_inc(S["scan_prep"], 1)
                dve.wait_ge(S["scan_prep"], a.upto(2, 1))
                dve.memset(starts, 0.0).then_inc(S["scan_prep"], 1)
                dve.wait_ge(S["scan_prep"], a.upto(2))
                dve.tensor_tensor_scan(ff[:], ff[:], resets[:], 0.0, ALU.mult, ALU.add).then_inc(S["scan_done"], 1)
                dve.wait_ge(S["scan_done"], a.upto(1))
                dve.tensor_copy(dmid[:], d[:, :, 0, HALF - 1]).then_inc(S["mid_done"], 1)
                dve.tensor_copy(dend[:], d[:, :, 1, HALF - 1]).then_inc(S["mid_done"], 1)
                dve.wait_ge(S["mid_done"], a.upto(3, 2))
                dve.reciprocal(rmid[:], dmid[:]).then_inc(S["rmid_done"], 1)
                dv, mv = dend[:].rearrange("p (h c) -> p h c", c=C), dmid[:].rearrange("p (h c) -> p h c", c=C)
                dve.tensor_tensor(gg[:], dv[:, :, 0:C - 1], mv[:, :, 1:C], ALU.mult).then_inc(S["mid_done"], 1)
                dve.wait_ge(S["rmid_done"], a.upto(1))
                dve.tensor_tensor(d[:, :, 0, :], d[:, :, 0, :], rmid[:].unsqueeze(2).broadcast_to((P, NH * C, HALF)), ALU.mult)\
                    .then_inc(S["e_done"], 1)

            def keys_queries(a):
                for h in range(NH):
                    dve.wait_ge(S["sig_q"], a.upto(NH, h + 1))
                    dve.scalar_tensor_tensor(out=qq[:, h], in0=bank(2 + h), scalar=1 / (SX * SW), in1=qq[:, h],
                                             op0=ALU.mult, op1=ALU.mult).then_inc(S["q_done"], 1)
                dve.wait_ge(S["q_done"], a.upto(NH))
                dve.wait_ge(S["e_done"], a.upto(1))
                dve.tensor_tensor(flat(qt)[:, a.par * NH * L:(a.par + 1) * NH * L], flat(qq), ff[:], ALU.mult).then_inc(S["qt_ready"], 1)
                dve.wait_ge(S["qt_ready"], a.upto(1))
                dve.reciprocal(ff[:], ff[:]).then_inc(S["re_done"], 1)
                dve.wait_ge(S["re_done"], a.upto(1))
                dve.tensor_tensor(flat(kk), flat(kk), ff[:], ALU.mult).then_inc(S["kt_ready"], 1)

            def masks(b):
                wait(dve, "ot_done", b.upto(NH, 0))
                m = const("mask")
                for h in range(NH):
                    dve.wait_ge(S["a_done"], b.upto(NH, h + 1))
                    sc = bank(4 + h).rearrange("p (c t) -> p c t", t=P)
                    dve.tensor_tensor(at[0:HALF, h], sc[0:HALF], m[0:HALF].unsqueeze(1).broadcast_to((HALF, C, P)), ALU.mult)\
                        .then_inc(S["at_ready"], 1)
                    dve.tensor_tensor(at[HALF:P, h, :, HALF:P], sc[HALF:P, :, HALF:P],
                                      m[HALF:P, HALF:P].unsqueeze(1).broadcast_to((HALF, C, HALF)), ALU.mult).then_inc(S["at_ready"], 1)

            def states(b):
                dve.wait_ge(S["kv_done"], b.upto(1))
                kv = ps[:, 4:4 + NH, :]
                g = lambda c: gg[:, :, c:c + 1].broadcast_to((P, NH, P))
                dve.tensor_tensor(sm[:, 0], kv[:, :, 0:P], g(0), ALU.mult).then_inc(S["sm_ready"], 1)
                for c in (1, 2):
                    dve.wait_ge(S["sm_ready"], b.upto(5, 2 * c - 1))
                    dve.tensor_tensor(smt[:], kv[:, :, c * P:(c + 1) * P], sm[:, c - 1], ALU.add).then_inc(S["sm_ready"], 1)
                    dve.wait_ge(S["sm_ready"], b.upto(5, 2 * c))
                    dve.tensor_tensor(sm[:, c], smt[:], g(c), ALU.mult).then_inc(S["sm_ready"], 1)

            def low2(z):
                dve.wait_ge(S["rowhi_ready"], z.upto(1))
                dve.tensor_tensor(rows[:, z.par, :, D:2 * D], xn2[:], rows[:, z.par, :, 0:D], ALU.subtract).then_inc(S["rowlo_ready"], 1)

            def over_experts(v):
                return v.unsqueeze(2).broadcast_to((P, C, E))

            def over_tokens(v):
                return v.unsqueeze(1).broadcast_to((P, C, E))

            def chain(name, z, per):
                k = [0]

                def step(ins, hold=True):
                    ins.then_inc(S[name], 1)
                    k[0] += 1
                    if hold:
                        dve.wait_ge(S[name], z.upto(per, k[0]) if z else k[0])
                    return k[0]
                return step, k

            def route_a(z):
                dve.wait_ge(S["lg_done"], z.upto(1))
                step, k = chain("route_a", z, ROUTE_A)
                logits = bank(5)[:, 0:C * E].rearrange("p (c e) -> p c e", e=E)
                for n, src in ((0, logits), (1, rt[:, 2])):
                    step(dve.tensor_reduce(rc[:, 2 * n], src, AX, ALU.max))
                    step(dve.tensor_tensor(rt[:, 0], src, over_experts(rc[:, 2 * n]), ALU.is_equal))
                    step(dve.tensor_tensor(rt[:, 0], rt[:, 0], over_tokens(const("tie")), ALU.mult))
                    step(dve.tensor_reduce(rc[:, 2 * n + 1], rt[:, 0], AX, ALU.max))
                    step(dve.tensor_tensor(rt[:, 1 + 2 * n], rt[:, 0], over_experts(rc[:, 2 * n + 1]), ALU.is_equal))
                    if n == 0:
                        step(dve.scalar_tensor_tensor(out=rt[:, 2], in0=rt[:, 1], scalar=-3e38, in1=logits, op0=ALU.mult, op1=ALU.add))
                step(dve.tensor_tensor(rc[:, 6], rc[:, 0], rc[:, 2], ALU.subtract), hold=False)
                step(dve.tensor_tensor(msel[:], rt[:, 1], rt[:, 3], ALU.add), hold=False)
                assert k[0] == ROUTE_A

            def route_b(z):
                dve.wait_ge(S["rk_done"], z.upto(1))
                step, k = chain("route_b", z, ROUTE_B)
                rank = bank(5)[:, 64:64 + C * E].rearrange("p (c e) -> p c e", e=E)
                step(dve.tensor_tensor(rt[:, 4], rank, over_tokens(cnt[:]), ALU.add))
                step(dve.tensor_tensor(cnt[:], cnt[:], bank(5)[:, 128:128 + E], ALU.add))
                for n in range(2):
                    step(dve.tensor_tensor(rt[:, 5], rt[:, 4], rt[:, 1 + 2 * n], ALU.mult))
                    step(dve.tensor_reduce(rc[:, 4 + n], rt[:, 5], AX, ALU.add))
                step(dve.tensor_copy(dest[:, z.par], rc[:, 4:6]), hold=False)
                dve.wait_ge(S["wsig_ready"], z.upto(2))
                words = rows32[:, z.par]
                step(dve.tensor_scalar(words[:, :, D + 3], rc[:, 1], -1.0, float(E), ALU.mult, ALU.add), hold=False)
                step(dve.tensor_scalar(words[:, :, D + 1], wsig[:, 1], 1 / (SH * SW), None, ALU.mult))
                step(dve.scalar_tensor_tensor(out=words[:, :, D + 2], in0=wsig[:, 0], scalar=1 / (SH * SW), in1=words[:, :, D + 1],
                                              op0=ALU.mult, op1=ALU.subtract), hold=False)
                assert k[0] == ROUTE_B

            def residual(b):
                dve.wait_ge(S["rms_ready"], b.upto(1))
                dve.wait_ge(S["xr_in"], b.upto(16))
                for c in range(C):
                    if c % 2 == 0:
                        dve.wait_ge(S["y_done"], b.upto(2, c // 2 + 1))
                    dve.scalar_tensor_tensor(out=xr[:, c], in0=bank(c // 2)[:, c % 2 * D:(c % 2 + 1) * D], scalar=rms[:, c:c + 1],
                                             in1=xr[:, c], op0=ALU.mult, op1=ALU.add).then_inc(S["x2_ready"], 1)
                dve.wait_ge(S["x2_ready"], b.upto(C))
                row_stats(b, xr, st2, mv2, "ln2_stats", "ln2_mv")

            def normalise2(b):
                dve.wait_ge(S["rstd2"], b.upto(1))
                wait(dve, "x2t_done", b.upto(KD, 0))
                for c in range(C):
                    dve.tensor_scalar(xn2[:, c], xr[:, c], mv2[:, c, 0:1], rs2[:, c:c + 1], ALU.subtract, ALU.mult)\
                        .then_inc(S["xn2_ready"], 1)

            def one(j, c, f=True, r=True, b_=True, s=True):
                a, b, z = Seq(j, c + 1), Seq(j, c), Seq(j, c - 1)
                if b_:
                    masks(b)
                if r:
                    low2(z)
                if f:
                    normalise1(a)
                if b_:
                    states(b)
                if f:
                    low1(a)
                if r:
                    route_a(z)
                if f:
                    decays(a)
                    keys_queries(a)
                if r:
                    route_b(z)
                if b_:
                    dve.wait_ge(S["ss_done"], b.upto(1))
                    dve.tensor_scalar(ssv[:], bank(4)[:, 0:C], 1 / D, EPS_RMS, ALU.mult, ALU.add).then_inc(S["ssv_ready"], 1)
                    residual(b)
                if s:
                    stats1(Seq(j, c + 2))
                if b_:
                    normalise2(b)

            step, k = chain("setup", None, 0)
            step(dve.memset(resets[:], 0.0), hold=False)
            step(dve.memset(at[HALF:P, :, :, 0:HALF], 0.0), hold=False)
            step(dve.memset(ones2[:], SW), hold=False)
            stats1(Seq(0, 0))
            dve.wait_ge(S["const_in"], 32)
            dve.wait_ge(S["small_in"], 64)
            dve.wait_ge(S["wo_in"], 32)
            step(dve.tensor_copy(cnt[:], const("base")), hold=False)
            for h in range(NH):
                step(dve.tensor_scalar(wos[:, h], wos[:, h], nws[:, h:h + 1], None, ALU.mult), hold=False)
            b1v = b1s[:].rearrange("p (e g j) -> p e g j", g=2, j=FJ)
            step(dve.tensor_scalar(b1v[:, :, 0], b1v[:, :, 0], ALPHA, None, ALU.mult), hold=False)
            step(dve.tensor_scalar(b1v[:, :, 1], b1v[:, :, 1], 1.0, SH / ALPHA, ALU.add, ALU.mult), hold=False)
            b2v = flat(vv)[0:2, :]
            step(dve.tensor_scalar(b2v, b2v, SH, None, ALU.mult))
            step(dve.tensor_copy(b2s[:], b2v))
            step(dve.scalar_tensor_tensor(out=b2s[:], in0=b2s[:], scalar=cfs[0:2, CF["low"][0]:CF["low"][1]], in1=b2v,
                                          op0=ALU.mult, op1=ALU.add), hold=False)
            dve.wait_ge(S["zero_out"], 16)
            step(dve.memset(resets[:, 0:1], 0.0), hold=False)
            assert k[0] == SETUP
            dve.wait_ge(S["split_high"], 2)
            dve.tensor_tensor(wp[:, 1].rearrange("p q k d -> p (q k d)"), wq_stage, wp[:, 0].rearrange("p q k d -> p (q k d)"),
                              ALU.subtract).then_inc(S["split_low"], 1)

            one(0, -1, r=False, b_=False)
            one(0, 0, r=False)
            pipelined(dve, 1, 4, one)
            one(0, 5)
            one(0, 6, s=False)
            one(0, 7, f=False, s=False)
            one(0, 8, f=False, b_=False, s=False)

            step, k = chain("plan_done", None, 0)
            ptile = flat(x2T)[:, 0:3 * NT * E].rearrange("p (a t e) -> p a t e", a=3, e=E)
            cols = lambda v: v.unsqueeze(1).broadcast_to((P, NT, E))
            tiles = lambda v: v.unsqueeze(2).broadcast_to((P, NT, E))
            step(dve.tensor_copy(plani[:, 2], cnt[:]))
            step(dve.tensor_tensor(plan[:, 0], cnt[:], const("base"), ALU.subtract))
            step(dve.tensor_scalar(plani[:, 0], plan[:, 0], float(RT - 1), None, ALU.add))
            step(dve.tensor_scalar(plani[:, 1], plani[:, 0], RT.bit_length() - 1, None, ALU.logical_shift_right))
            step(dve.tensor_copy(plan[:, 0], plani[:, 1]))
            step(dve.tensor_tensor_scan(plan[:, 1], const("ones"), plan[:, 0], 0.0, ALU.mult, ALU.add))
            step(dve.tensor_tensor(plan[:, 2], plan[:, 1], plan[:, 0], ALU.subtract))
            step(dve.scalar_tensor_tensor(out=plan[:, 3], in0=plan[:, 2], scalar=-float(RT), in1=const("base"),
                                          op0=ALU.mult, op1=ALU.add))
            step(dve.tensor_tensor(ptile[:, 0], cols(plan[:, 1]), tiles(const("tile")), ALU.is_le))
            step(dve.tensor_reduce(pt[:, 0], ptile[:, 0], AX, ALU.add))
            step(dve.tensor_tensor(ptile[:, 1], tiles(pt[:, 0]), cols(const("eidx")), ALU.is_equal))
            step(dve.tensor_tensor(ptile[:, 2], ptile[:, 1], cols(plan[:, 3]), ALU.mult))
            step(dve.tensor_reduce(pt[:, 1], ptile[:, 2], AX, ALU.add))
            step(dve.tensor_scalar(pt[:, 2], pt[:, 0], float(E), None, ALU.is_lt))
            step(dve.tensor_tensor(pt[:, 3], pt[:, 2], const("tile_row"), ALU.mult))
            step(dve.tensor_tensor(pt[:, 1], pt[:, 1], pt[:, 3], ALU.add))
            step(dve.tensor_scalar(roff[:], pt[:, 1], float(SPARE), None, ALU.add), hold=False)
            step(dve.tensor_scalar(etab[:], pt[:, 0], float(E - 1), None, ALU.min), hold=False)
            assert k[0] == PLAN

            def tile(j, c, u=True, d=True):
                i, z = Seq(j, c), Seq(j, c - 1)
                if u:
                    h = flat(xs)[:, 0:FJ * RT]
                    v, g = (t(i).rearrange("p q t -> p (q t)") for t in (value_of, silu_of))
                    hi, lo = (hhl(i)[:, n].rearrange("p q t -> p (q t)") for n in range(2))
                    dve.wait_ge(S["sv_ready"], i.upto(2 * FJ))
                    dve.tensor_scalar(v, v, (LIMIT + 1) * SH / ALPHA, (1 - LIMIT) * SH / ALPHA, ALU.min, ALU.max).then_inc(S["h_ready"], 1)
                    dve.wait_ge(S["h_ready"], i.upto(4, 1))
                    dve.scalar_tensor_tensor(out=h, in0=g, scalar=SILU_MAX, in1=v, op0=ALU.min, op1=ALU.mult).then_inc(S["h_ready"], 1)
                    dve.wait_ge(S["h_ready"], i.upto(4, 2))
                    wait(dve, "g2_done", i.upto(1, -1))
                    dve.tensor_copy(hi, h).then_inc(S["h_ready"], 1)
                    dve.wait_ge(S["h_ready"], i.upto(4, 3))
                    dve.tensor_tensor(lo, h, hi, ALU.subtract).then_inc(S["h_ready"], 1)
                if d:
                    dve.wait_ge(S["g2_done"], z.upto(1))
                    dve.wait_ge(S["w_ready"], z.upto(WSTEPS))
                    wait(dve, "added", z.upto(32, -32))
                    for s in range(SR):
                        dve.tensor_scalar(y_of(z)[:, s], bank(6 + z.par)[:, s * D:(s + 1) * D], wrow[:, z.par, 1, s:s + 1], None,
                                          ALU.mult).then_inc(S["y_ready"], 1)

            tile(0, 0, d=False)
            for c in range(1, 4):
                tile(0, c)
            pipelined(dve, 4, NT - 2, tile)
            tile(0, NT - 1)
            tile(0, NT, u=False)

        @block.gpsimd
        def _(pool):
            pool.wait_ge(S["const_in"], 32)

            def rstd(b, mv_, var_sem, out_, out_sem, mv_sem):
                wait_apart(pool, (S[mv_sem], b.upto(C)))
                pool.tensor_scalar(pw[:, 0], mv_[:, :, 1], EPS_LN, None, ALU.add).then_inc(S[var_sem], 1)
                pool.wait_ge(S[var_sem], b.upto(2, 1))
                pool.tensor_tensor(pw[:, 1], pw[:, 0], const("half"), ALU.pow).then_inc(S[var_sem], 1)
                wait_apart(pool, (S[var_sem], b.upto(2)))
                pool.tensor_scalar(out_[:], pw[:, 1], SX, None, ALU.mult).then_inc(S[out_sem], 1)

            def one(j, c, r=True, b_=True, s=True):
                b, z = Seq(j, c), Seq(j, c - 1)
                if b_:
                    for q in range(CPS):
                        m, slot = b.n * CPS + q, (CPS * c + q) % 2
                        pool.wait_ge(S["we_high"], m + 1)
                        pool.tensor_tensor(wes[:, 1, bass.ds(m * WCH, WCH)], wst[:, slot], wes[:, 0, bass.ds(m * WCH, WCH)],
                                           ALU.subtract).then_inc(S["we_low"], 1)
                if r:
                    wait_apart(pool, ("rowhi_ready", z.upto(1)))
                    at_ = CF["tok"][0]
                    pool.tensor_copy(rows_i[:, z.par, :, D], cfs[:].bitcast(I32)[:, bass.ds(z.n * C + at_, C)]).then_inc(S["tok_ready"], 1)
                if b_:
                    pool.wait_ge(S["ssv_ready"], b.upto(1))
                    pool.tensor_tensor(rms[:], ssv[:], const("half"), ALU.pow).then_inc(S["rms_ready"], 1)
                    rstd(b, mv2, "ln2_var", rs2, "rstd2", "ln2_mv")
                if s:
                    rstd(Seq(j, c + 2), mv1, "ln1_var", rs1, "rstd1", "ln1_mv")
                if r:
                    wait_apart(pool, ("route_b", z.upto(ROUTE_B)), ("rowlo_ready", z.upto(1)), ("tok_ready", z.upto(1)))
                    for c_ in range(C):
                        for n in range(2):
                            pool.indirect_dma_start(rows_dram, bass.IndirectOffsetOnAxis(ap=dest[:, z.par, n, c_:c_ + 1], axis=0),
                                                    rows_i[:, z.par, c_, :], None).then_inc(disp[z.par], 16)

            rstd(Seq(0, 0), mv1, "ln1_var", rs1, "rstd1", "ln1_mv")
            one(0, -1, r=False, b_=False)
            one(0, 0, r=False)
            pipelined(pool, 1, 4, one)
            one(0, 5)
            one(0, 6, s=False)
            one(0, 7, s=False)
            one(0, 8, b_=False, s=False)

            pool.wait_ge(S["plan_done"], PLAN)
            pool.wait_ge(S["x2_out"], 16 * NSEQ)
            pool.wait_ge(S["zero_out"], 16)

            def tile(j, c, u=True, d=True):
                i, z = Seq(j, c), Seq(j, c - 1)
                if u:
                    wait_apart(pool, (xg_in[i.par], i.upto_half(16)),
                                     ("added", i.upto(32, -32)))
                    m = meta[:, i.par]
                    pool.tensor_copy(token[:, i.par], rows_i[:, i.par, 0:SR, D]).then_inc(S["meta_ready"], 1)
                    pool.tensor_copy(m, rows32[:, i.par, 0:SR, D + 1:D + 4]).then_inc(S["meta_ready"], 1)
                    pool.wait_ge(S["meta_ready"], i.upto(2))
                    ef = pt[:, 0, bass.ds(i.n, 1)].broadcast_to((P, SR))
                    same, w = wrow[:, i.par, 0], wrow[:, i.par, 1]
                    pool.tensor_tensor(same, m[:, :, 2], ef, ALU.subtract).then_inc(S["w_ready"], 1)
                    wait_apart(pool, ("w_ready", i.upto(WSTEPS, 1)))
                    pool.tensor_scalar(same, same, 0.0, None, ALU.is_equal).then_inc(S["w_ready"], 1)
                    pool.wait_ge(S["w_ready"], i.upto(WSTEPS, 2))
                    pool.tensor_tensor(w, same, m[:, :, 1], ALU.mult).then_inc(S["w_ready"], 1)
                    pool.wait_ge(S["w_ready"], i.upto(WSTEPS, 3))
                    pool.tensor_tensor(w, w, m[:, :, 0], ALU.add).then_inc(S["w_ready"], 1)
                if d:
                    wait_apart(pool, ("y_ready", z.upto(SR)),
                                     ("added", z.upto(32, 0)))
                    for s in range(SR):
                        pool.indirect_dma_start(out, bass.IndirectOffsetOnAxis(ap=token[:, z.par, s:s + 1], axis=0),
                                                y_of(z)[:, s], None, compute_op=ALU.add).then_inc(S["added"], 16)

            tile(0, 0, d=False)
            tile(0, 1)
            pipelined(pool, 2, NT - 2, tile)
            tile(0, NT - 1)
            tile(0, NT, u=False)


def constants():
    import numpy as np

    cf = np.zeros((P, CFN), np.float32)
    p = np.arange(P)

    def put(name, v):
        a, b = CF[name]
        cf[:, a:b] = v

    put("ident", np.eye(P))
    put("mask", p[:, None] <= p[None, :])
    put("base", np.arange(E) * REGION)
    put("tie", E - np.arange(E))
    put("eidx", np.arange(E))
    put("tile", np.arange(NT))
    put("tile_row", np.arange(NT) * RT - SPARE)
    put("half", -0.5)
    put("ones", 1.0)
    put("low", -1.0 * (p[:, None] == 1))
    a, b = CF["tok"]
    cf[:, a:b].view(np.int32)[:] = np.arange(T // P)[None, :] * P + p[:, None]
    ch = np.concatenate([np.eye(P), p[:, None] < p[None, :], np.ones((P, P))], 1).astype(np.float16)
    words = np.zeros((P, SR, WORDS), np.int32)
    words[:, :, D] = T + np.arange(SR)[None, :] * P + p[:, None]
    words[:, :, D + 3] = np.float32(-1.0).view(np.int32)
    return cf, ch, words


def kernel(L0_attn_x, L0_attn_Wq, L0_attn_Wk, L0_attn_Wv, L0_attn_Wo, L0_attn_norm_w, L0_ffn_gate_w,
           L0_ffn_dense_1_w, L0_ffn_dense_1_b, L0_ffn_dense_2_w, L0_ffn_dense_2_b):
    import numpy as np
    import concourse.bacc as bacc
    from concourse.bass_utils import run_bass_kernel_spmd

    def halves(w):
        return np.asarray(w).T.reshape(KD, P, D).transpose(1, 0, 2)

    x = np.ascontiguousarray(np.asarray(L0_attn_x).reshape(T, D))
    wqkv = np.stack([halves(w) for w in (L0_attn_Wq, L0_attn_Wk, L0_attn_Wv)], 1).reshape(P, 3 * KD * D)
    wo = np.ascontiguousarray(halves(L0_attn_Wo))
    norm_w = np.ascontiguousarray(np.asarray(L0_attn_norm_w).reshape(NH, P).T)
    gate_w = np.ascontiguousarray(np.asarray(L0_ffn_gate_w).reshape(KD, P, E).transpose(1, 0, 2))
    w1 = np.asarray(L0_ffn_dense_1_w).reshape(E, FF, 2, KD, P).transpose(4, 0, 3, 2, 1).reshape(P, W1COLS)
    w2 = np.asarray(L0_ffn_dense_2_w).reshape(E, D, FJ, P).transpose(3, 0, 2, 1).reshape(P, W2COLS)
    we = np.concatenate([w1, w2], 1)
    b1 = np.ascontiguousarray(np.asarray(L0_ffn_dense_1_b).reshape(E, FJ, P, 2).transpose(2, 0, 3, 1).reshape(P, E * 2 * FJ))
    b2 = np.ascontiguousarray(np.asarray(L0_ffn_dense_2_b).reshape(1, E * D))
    cf, ch, pad = constants()
    arrays = dict(x=x, wqkv=wqkv, wo=wo, norm_w=norm_w, gate_w=gate_w, we=we, b1=b1, b2=b2, cf=cf, ch=ch, pad=pad)

    nc = bacc.Bacc("TRN2", target_bir_lowering=False, num_devices=1)
    args = [nc.dram_tensor(n, a.shape, mybir.dt.from_np(a.dtype), kind="ExternalInput").ap() for n, a in arrays.items()]
    args.append(nc.dram_tensor("out", (T + RT, D), F32, kind="ExternalOutput").ap())
    build_kernel(nc, *args)
    got = run_bass_kernel_spmd(nc, [arrays], core_ids=[0]).results[0]["out"]
    return got[0:T].reshape(NSEQ, L, D)
```

```python
import math
from contextlib import ExitStack

import concourse.bass as bass
from concourse import mybir

ALU = mybir.AluOpType
ACT = mybir.ActivationFunctionType
AX = mybir.AxisListType.X
F32 = mybir.dt.float32
F16 = mybir.dt.float16
I32 = mybir.dt.int32

P = 128
NSEQ, L, D = 8, 512, 256
T = NSEQ * L
C = L // P
KD = D // P
NH = KD
HALF = P // 2
E, FF = 8, 512
FJ = FF // P
RT = 256
SR = RT // P
REGION = T + RT
SPARE = E * REGION
NT = 2 * T // RT + E - 1
ROW = 2 * D + 8
WORDS = ROW // 2

SX = 2.0 ** 11
SW = 2.0 ** 8
SH = 2.0 ** 8
ALPHA, LIMIT = 1.702, 9.0
SILU_MAX = ALPHA * LIMIT / (1 + math.exp(-ALPHA * LIMIT))
EPS_LN, EPS_RMS = 1e-5, 1e-6
WCH = 1024
W1COLS, W2COLS = E * KD * 2 * FF, E * FJ * D
NCH = (W1COLS + W2COLS) // WCH
CPS = NCH // NSEQ
SETUP, ROUTE_A, ROUTE_B, PLAN, WSTEPS = 12, 13, 10, 18, 4

CF = {}
_at = 0
for _name, _n in (("ident", P), ("mask", P), ("base", E), ("tie", E), ("eidx", E), ("tile", NT), ("tile_row", NT),
                  ("half", C), ("ones", E), ("low", 1), ("tok", T // P)):
    CF[_name] = (_at, _at + _n)
    _at += _n
CFN = _at


class Seq:

    def __init__(self, j, c, unroll=2):
        self.j, self.c = j, c
        self.n = unroll * j + c
        self.par = c % 2
        self.half = unroll // 2 * j + c // 2

    def upto(self, per, count=None):
        return self.n * per + (per if count is None else count)

    def upto_half(self, per):
        return self.half * per + per


class Tile(Seq):

    def __init__(self, j, c):
        super().__init__(j, c, 4)
        self.slot = c % 4
        self.turn = j + c // 4


def build_kernel(nc, x, wqkv, wo, norm_w, gate_w, we, b1, b2, cf, ch, pad, out):
    rows_dram = nc.dram_tensor("dispatched_rows", (SPARE + REGION, WORDS), I32).ap()

    with ExitStack() as ctx:
        def sb(name, shape, dt=F32):
            return ctx.enter_context(nc.sbuf_tensor(name, shape, dt))

        def sem(name):
            return ctx.enter_context(nc.semaphore(name))

        wes = sb("wes", [P, 2, W1COLS + W2COLS], F16)
        wst = sb("wst", [P, 2, WCH])
        wp = sb("wp", [P, 2, 3, KD, D], F16)
        wos = sb("wos", [P, NH, D])
        nws = sb("nws", [P, NH])
        gws = sb("gws", [P, KD, E])
        b1s = sb("b1s", [P, E * 2 * FJ])
        b2s = sb("b2s", [2, E * D], F16)
        ones2 = sb("ones2", [2, P], F16)
        cfs = sb("cfs", [P, CFN])
        chs = sb("chs", [P, 3 * P], F16)
        xs = sb("xs", [P, 2, C, D])
        xr = sb("xr", [P, C, D])
        xhl = sb("xhl", [P, 2, C, D], F16)
        xT = sb("xT", [P, 2, KD, L], F16)
        ff = sb("ff", [P, NH * L])
        kk = sb("kk", [P, NH, L])
        qq = sb("qq", [P, NH, L])
        resets = sb("resets", [P, NH * L])
        qt = sb("qt", [P, 2, NH, L])
        vv = sb("vv", [P, 2, C, D])
        at = sb("at", [P, NH, C, P])
        kTs = sb("kTs", [P, NH, C - 1, P])
        sm = sb("sm", [P, C - 1, NH, P])
        smt = sb("smt", [P, NH, P])
        ots = sb("ots", [P, NH, L])
        xn2 = sb("xn2", [P, C, D])
        x2T = sb("x2T", [P, KD, L])
        rows = sb("rows", [P, 2, C, ROW], F16)
        st = sb("st", [P, C, 6])
        st2 = sb("st2", [P, C, 6])
        mv1 = sb("mv1", [P, C, 2])
        mv2 = sb("mv2", [P, C, 2])
        pw = sb("pw", [P, 4, C])
        rs1 = sb("rs1", [P, C])
        rms = sb("rms", [P, C])
        rs2 = sb("rs2", [P, C])
        ssv = sb("ssv", [P, C])
        dmid = sb("dmid", [P, NH * C])
        dend = sb("dend", [P, NH * C])
        rmid = sb("rmid", [P, NH * C])
        gg = sb("gg", [P, NH, C - 1])
        rt = sb("rt", [P, 6, C, E])
        rc = sb("rc", [P, 8, C])
        msel = sb("msel", [P, C, E], F16)
        wsig = sb("wsig", [P, 2, C])
        cnt = sb("cnt", [P, E])
        dest = sb("dest", [P, 2, 2, C], I32)
        plan = sb("plan", [P, 4, E])
        plani = sb("plani", [P, 3, E], I32)
        pt = sb("pt", [P, 4, NT])
        roff = sb("roff", [P, NT], I32)
        etab = sb("etab", [P, NT], I32)
        pads = sb("pads", [P, SR, WORDS], I32)
        meta = sb("meta", [P, 4, SR, 3])
        token = sb("token", [P, 4, SR], I32)
        wrow = sb("wrow", [P, 4, 2, SR])

        ps = ctx.enter_context(nc.psum_tensor("ps", [P, 8, 512], F32))

        def bank(i):
            return ps[:, i, :]

        def bank16(i):
            return ps[:, i, :].bitcast(F16)

        def const(name):
            a, b = CF[name]
            return cfs[:, a:b]

        identh, upper, ones16 = chs[:, 0:P], chs[:, P:2 * P], chs[:, 2 * P:3 * P]
        ident = const("ident")

        names = """x_in0 x_in1 xr_in x2_out small_in wq_in wo_in const_in st_in0 st_in1 pads_in pad_out zero_out
            setup split_high split_low we_scaled we_high we_low
            ln1_stats ln1_mv ln1_var rstd1 xn_ready xh_ready xl_ready t1_done xT_ready kp_done qp_done vp_done
            sig_k dec_ready sig_q v_ready scan_prep scan_done mid_done rmid_done e_done q_done qt_ready re_done kt_ready
            a_done at_ready kt_done kts_ready kv_done sm_ready ot_done ots_ready sq_ready ss_done ssv_ready rms_ready
            y_done x2_ready ln2_stats ln2_mv ln2_var rstd2 xn2_ready rowhi_ready rowlo_ready x2t_done x2T_ready lg_done
            route_a wsig_ready rk_done route_b tok_ready disp0 disp1 plan_done
            xg_in0 xg_in1 xg_in2 xg_in3 tx_done xtc_ready g1_done sv_ready h_ready g2_done y_ready meta_ready w_ready added held""".split()
        S = {n: sem(n) for n in names}
        x_in, disp, st_in = ([S[f"{n}{i}"] for i in range(2)] for n in ("x_in", "disp", "st_in"))
        xg_in = [S[f"xg_in{i}"] for i in range(4)]

        rows32 = rows[:].bitcast(F32)
        rows_i = rows[:].bitcast(I32)
        wq_stage = qt[:].rearrange("p a h l -> p (a h l)")[:, 0:3 * KD * D]

        def flat(t):
            names = " ".join("abcde"[:len(t.shape) - 1])
            return t[:].rearrange(f"p {names} -> p ({names})") if len(t.shape) > 2 else t[:]

        def row_buffer(t, i):
            return t[:, i.slot // 2, i.slot % 2 * SR:(i.slot % 2 + 1) * SR]

        def xTm(i):
            return flat(xT)[:, i.par * 4 * RT:(i.par + 1) * 4 * RT].rearrange("p (q t) -> p q t", t=RT)

        def silu_of(i):
            return flat((kk, qq)[i.par]).rearrange("p (q t) -> p q t", t=RT)

        def value_of(i):
            return flat((ff, at)[i.par]).rearrange("p (q t) -> p q t", t=RT)

        def hhl(i):
            return flat((ots, xn2)[i.par]).bitcast(F16).rearrange("p (a q t) -> p a q t", a=2, t=RT)

        def y_of(i):
            return flat(x2T)[:, i.par * SR * D:(i.par + 1) * SR * D].rearrange("p (s d) -> p s d", d=D)

        block = ctx.enter_context(nc.Block())

        x_v = x.rearrange("(s p) d -> p s d", p=P)
        out_v = out.rearrange("(s p) d -> p s d", p=P)

        def wait(eng, name, value):
            if isinstance(value, int) and value <= 0:
                return
            eng.wait_ge(S[name] if isinstance(name, str) else name, value)

        def wait_apart(eng, *waits):
            for name, v in waits:
                wait(eng, name, v)
                if not isinstance(v, int):
                    eng.sem_inc(S["held"], 1)

        def pipelined(eng, first, last, one, unroll=2):
            assert (last - first + 1) % unroll == 0
            with eng.Fori(0, (last - first + 1) // unroll) as j:
                for u in range(unroll):
                    one(j, first + u)

        def stages(c):
            return [0 <= q < NSEQ for q in (c + 2, c + 1, c, c - 1)]

        def iterations(eng, one):
            for c in (-2, -1, 0):
                one(0, c)
            pipelined(eng, 1, 4, one)
            for c in range(5, NSEQ + 1):
                one(0, c)

        @block.sync
        def _(sp):
            sp.dma_start(cfs[:], cf).then_inc(S["const_in"], 16)
            sp.dma_start(xs[:, 0], x_v[:, 0:C]).then_inc(x_in[0], 16)
            sp.dma_start(chs[:], ch).then_inc(S["const_in"], 16)
            sp.dma_start(qt[:].rearrange("p a h l -> p (a h l)")[:, 0:3 * KD * D], wqkv).then_inc(S["wq_in"], 16)
            sp.dma_start(xs[:, 1], x_v[:, C:2 * C]).then_inc(x_in[1], 16)
            sp.dma_start(wos[:], wo).then_inc(S["wo_in"], 16)
            sp.dma_start(nws[:], norm_w).then_inc(S["wo_in"], 16)
            sp.dma_start(gws[:], gate_w).then_inc(S["small_in"], 16)
            sp.dma_start(b1s[:], b1).then_inc(S["small_in"], 16)
            for p in range(2):
                sp.dma_start(vv[p:p + 1].rearrange("p a c d -> p (a c d)"), b2).then_inc(S["small_in"], 16)
            sp.dma_start(pads[:], pad).then_inc(S["pads_in"], 16)
            sp.dma_start(xr[:], x_v[:, 0:C]).then_inc(S["xr_in"], 16)
            sp.wait_ge(S["pads_in"], 16)
            sp.dma_start(rows_dram[SPARE:SPARE + RT, :].rearrange("(s p) n -> p s n", p=P), pads[:]).then_inc(S["pad_out"], 16)
            sp.wait_ge(S["setup"], 1)
            sp.dma_start(out_v[:, T // P:T // P + SR, :], resets[:, 0:SR * D].rearrange("p (s d) -> p s d", d=D)).then_inc(S["zero_out"], 16)

            def weights_in(m, slot):
                wait_apart(sp, ("we_low", m - 1))
                sp.dma_start(wst[:, slot], we[:, bass.ds(m * WCH, WCH)]).then_inc(st_in[slot], 16)

            weights_in(0, 0)
            weights_in(1, 1)

            def one(j, c, load=True, keep=True):
                b = Seq(j, c)
                if load:
                    a = Seq(j, c + 2)
                    wait_apart(sp, ("xl_ready", b.upto(1)),
                                   ("ss_done", b.upto(1, 0)))
                    sp.dma_start(xs[:, a.par], x_v[:, bass.ds(a.n * C, C)]).then_inc(x_in[a.par], 16)
                for q in range(CPS if keep else CPS - 2):
                    weights_in(b.n * CPS + 2 + q, (CPS * c + q) % 2)
                wait_apart(sp, ("x2_ready", b.upto(C)))
                sp.dma_start(out_v[:, bass.ds(b.n * C, C)], xr[:]).then_inc(S["x2_out"], 16)
                if keep:
                    wait_apart(sp, ("x2_out", b.upto(16)), ("xn2_ready", b.upto(C)))
                    a = Seq(j, c + 1)
                    sp.dma_start(xr[:], x_v[:, bass.ds(a.n * C, C)]).then_inc(S["xr_in"], 16)

            one(0, 0)
            pipelined(sp, 1, 4, one)
            one(0, 5)
            one(0, 6, load=False)
            one(0, 7, load=False, keep=False)
            sp.wait_ge(S["plan_done"], PLAN)
            for e in range(E):
                row = sp.value_load(plani[0:1, 2, e:e + 1], min_val=0, max_val=SPARE - RT)
                sp.dma_start(rows_dram[bass.ds(row, RT), :].rearrange("(s p) n -> p s n", p=P), pads[:]).then_inc(S["pad_out"], 16)
            sp.wait_ge(S["pad_out"], 16 * (E + 1))
            for i in range(2):
                sp.wait_ge(disp[i], 16 * 2 * C * NSEQ // 2)

            def tile_in(j, c):
                i = Tile(j, c)
                wait_apart(sp, ("tx_done", i.upto(1, -3)),
                               ("meta_ready", i.upto(2, -6)))
                row = sp.value_load(roff[0:1, bass.ds(i.n, 1)], min_val=0, max_val=SPARE)
                sp.dma_start(row_buffer(rows_i, i), rows_dram[bass.ds(row, RT), :].rearrange("(s p) n -> p s n", p=P)).then_inc(xg_in[i.slot], 16)

            for c in range(7):
                tile_in(0, c)
            pipelined(sp, 7, NT - 1, tile_in, 4)
            sp.wait_ge(S["x2_out"], 16 * NSEQ)
            sp.wait_ge(S["zero_out"], 16)
            sp.wait_ge(S["added"], 32 * NT)


        @block.tensor
        def _(pe):
            def chunk(c):
                return slice(c * P, (c + 1) * P)

            def transposed_x(b, part):
                wait(pe, "xT_ready", b.upto(2, 0))
                wait(pe, "x2_ready", b.upto(C, -C))
                wait(pe, ("xh_ready", "xl_ready")[part], b.upto(1))
                for k in range(KD):
                    for c in range(C):
                        mm = pe.transpose(bank16(part)[:, k * L + c * P:k * L + (c + 1) * P],
                                          xhl[:, part, c, k * P:(k + 1) * P], identh)
                mm.then_inc(S["t1_done"], 1)

            def three(o, lhs, rhs):
                terms = [(k, a, c) for k in range(KD) for a, c in ((0, 0), (0, 1), (1, 0))]
                for n, (k, a, c) in enumerate(terms):
                    mm = pe.matmul(o, lhs(a, k), rhs(c, k), start=n == 0, stop=n == len(terms) - 1)
                return mm

            def project_heads(b, which, name):
                for h in range(NH):
                    if which == 1:
                        wait(pe, "v_ready", b.upto(2, h - 1))
                        if h == 0:
                            wait(pe, "xT_ready", b.upto(2))
                    else:
                        wait(pe, "sig_k", b.upto(2 * NH, 2 * h + 2))
                    three(bank(2 + h), lambda a, k: wp[:, a, which, k, h * P:(h + 1) * P],
                          lambda a, k: xT[:, a, k, :]).then_inc(S[name], 1)

            def project_v(b):
                for pair in range(2):
                    wait(pe, "q_done", b.upto(NH, pair + 1))
                    for c in range(2 * pair, 2 * pair + 2):
                        mm = three(bank(2 + pair)[:, c % 2 * D:(c % 2 + 1) * D],
                                   lambda a, k: xT[:, a, k, chunk(c)], lambda a, k: wp[:, a, 2, k, :])
                    mm.then_inc(S["vp_done"], 1)

            def scores(b):
                wait(pe, "kt_ready", b.upto(1))
                wait(pe, "qt_ready", b.upto(1))
                wait(pe, "ssv_ready", b.upto(1, 0))
                wait(pe, "route_b", b.upto(ROUTE_B, 2 - 2 * ROUTE_B))
                for h in range(NH):
                    for c in range(C):
                        mm = pe.matmul(bank(4 + h)[:, chunk(c)], kk[:, h, chunk(c)], qt[:, b.par, h, chunk(c)],
                                       start=True, stop=True)
                    mm.then_inc(S["a_done"], 1)

            def keys(b):
                for h in range(NH):
                    wait(pe, "sq_ready", b.upto(NH, h + 1 - NH))
                    for c in range(C - 1):
                        mm = pe.transpose(bank(6 + h)[:, chunk(c)], kk[:, h, chunk(c)], ident)
                    mm.then_inc(S["kt_done"], 1)

            def states(b):
                wait(pe, "at_ready", b.upto(2 * NH))
                wait(pe, "kts_ready", b.upto(NH))
                wait(pe, "v_ready", b.upto(2))
                for h in range(NH):
                    for c in range(C - 1):
                        mm = pe.matmul(bank(4 + h)[:, chunk(c)], kTs[:, h, c, :], vv[:, b.par, c, h * P:(h + 1) * P],
                                       start=True, stop=True)
                mm.then_inc(S["kv_done"], 1)

            def outputs(b):
                wait(pe, "sm_ready", b.upto(5))
                for h in range(NH):
                    for c in range(C):
                        mm = pe.matmul(bank(6 + h)[:, chunk(c)], vv[:, b.par, c, h * P:(h + 1) * P], at[:, h, c, :],
                                       start=True, stop=c == 0)
                        if c:
                            mm = pe.matmul(bank(6 + h)[:, chunk(c)], sm[:, c - 1, h, :], qt[:, b.par, h, chunk(c)],
                                           start=False, stop=True)
                    mm.then_inc(S["ot_done"], 1)

            def squares(b):
                wait(pe, "sq_ready", b.upto(NH))
                for c in range(C):
                    for h in range(NH):
                        mm = pe.matmul(bank(4)[:, c:c + 1], xs[:, 1 - b.par].rearrange("p c d -> p (c d)")[:, h * L + c * P:h * L + (c + 1) * P],
                                       const("ones")[:, 0:1], start=h == 0, stop=h == NH - 1)
                mm.then_inc(S["ss_done"], 1)

            def mixed(b, last):
                if not last:
                    wait(pe, "xT_ready", b.upto(2, 4))
                wait(pe, "x2T_ready", b.upto(KD, 0))
                for c in range(C):
                    for h in range(NH):
                        mm = pe.matmul(bank(c // 2)[:, c % 2 * D:(c % 2 + 1) * D], ots[:, h, chunk(c)], wos[:, h, :],
                                       start=h == 0, stop=h == NH - 1)
                    if c % 2:
                        mm.then_inc(S["y_done"], 1)

            def transposed_x2(b, last):
                wait(pe, "xn2_ready", b.upto(C))
                if not last:
                    wait(pe, "xT_ready", b.upto(2, 6))
                for k in range(KD):
                    for c in range(C):
                        mm = pe.transpose(bank(k)[:, chunk(c)], xn2[:, c, k * P:(k + 1) * P], ident)
                    mm.then_inc(S["x2t_done"], 1)

            def gates(b, last=False):
                wait(pe, "x2T_ready", b.upto(KD))
                if not last:
                    wait(pe, "sm_ready", b.upto(5, 10))
                for c in range(C):
                    for k in range(KD):
                        mm = pe.matmul(bank(5)[:, c * E:(c + 1) * E], x2T[:, k, chunk(c)], gws[:, k, :],
                                       start=k == 0, stop=k == KD - 1)
                mm.then_inc(S["lg_done"], 1)

            def ranks(b):
                wait(pe, "route_a", b.upto(ROUTE_A))
                for c in range(C):
                    for d in range(c + 1):
                        mm = pe.matmul(bank(5)[:, 64 + c * E:64 + (c + 1) * E], upper if d == c else ones16, msel[:, d, :],
                                       start=d == 0, stop=d == c)
                for d in range(C):
                    mm = pe.matmul(bank(5)[:, 128:128 + E], ones16, msel[:, d, :], start=d == 0, stop=d == C - 1)
                mm.then_inc(S["rk_done"], 1)

            def one(j, c):
                n, p, m, r = stages(c)
                a1, a, b, z = (Seq(j, c + 2 - q) for q in range(4))
                if r:
                    transposed_x2(z, last=not p)
                if p:
                    project_heads(a, 1, "kp_done")
                if r:
                    gates(z, last=not m)
                if m:
                    outputs(b)
                if r:
                    ranks(z)
                if p:
                    project_heads(a, 0, "qp_done")
                if m:
                    squares(b)
                    mixed(b, last=not p)
                if p:
                    project_v(a)
                    scores(a)
                    keys(a)
                if n:
                    transposed_x(a1, 0)
                if p:
                    states(a)
                if n:
                    transposed_x(a1, 1)

            pe.wait_ge(S["const_in"], 32)
            pe.wait_ge(S["small_in"], 64)
            pe.wait_ge(S["split_low"], 1)
            pe.wait_ge(S["setup"], SETUP)
            iterations(pe, one)

            def tile_transposed(i):
                wait(pe, xg_in[i.slot], i.turn * 16 + 16)
                wait(pe, "xtc_ready", i.upto(1, -1))
                for part in range(2):
                    for k in range(KD):
                        for s in range(SR):
                            mm = pe.transpose(bank16(4 + i.par)[:, (2 * part + k) * RT + s * P:(2 * part + k) * RT + (s + 1) * P],
                                              row_buffer(rows, i)[:, s, part * D + k * P:part * D + (k + 1) * P], identh)
                mm.then_inc(S["tx_done"], 1)

            def up(i, e):
                pe.wait_ge(S["xtc_ready"], i.upto(1))
                for j in range(FJ):
                    wait(pe, "sv_ready", i.upto(2 * FJ, 2 * j + 2 - 2 * FJ))
                    for g in range(2):
                        terms = [(k, a, c) for k in range(KD) for a, c in ((0, 0), (0, 1), (1, 0))]
                        for n, (k, a, c) in enumerate(terms):
                            lhs = wes[:, a, bass.ds(e * (KD * 2 * FF) + (k * 2 * FF + g * FF + j * P), P)]
                            mm = pe.matmul(bank(j)[:, g * RT:(g + 1) * RT], lhs, xTm(i)[:, 2 * c + k, :],
                                           start=n == 0, stop=n == len(terms) - 1)
                    mm.then_inc(S["g1_done"], 1)

            def down(i, e):
                pe.wait_ge(S["h_ready"], i.upto(4))
                wait(pe, "y_ready", i.upto(SR, -SR))
                for s in range(SR):
                    o = bank(6 + i.par)[:, s * D:(s + 1) * D]
                    pe.matmul(o, ones2[0:2, :], b2s[0:2, bass.ds(e * D, D)], start=True, stop=False)
                    for j in range(FJ):
                        for a, c in ((0, 0), (1, 0), (0, 1)):
                            rhs = wes[:, c, bass.ds(e * (FJ * D) + (W1COLS + j * D), D)]
                            mm = pe.matmul(o, hhl(i)[:, a, j, s * P:(s + 1) * P], rhs, start=False, stop=j == FJ - 1 and (a, c) == (0, 1))
                mm.then_inc(S["g2_done"], 1)

            def tile(j, c, t=True, u=True, d=True):
                i = Tile(j, c)
                if t:
                    tile_transposed(Tile(j, c + 1))
                if u:
                    up(i, pe.value_load(etab[0:1, bass.ds(i.n, 1)], min_val=0, max_val=E - 1))
                if d:
                    z = Tile(j, c - 1)
                    down(z, pe.value_load(etab[0:1, bass.ds(z.n, 1)], min_val=0, max_val=E - 1))

            tile(0, -1, u=False, d=False)
            tile(0, 0, d=False)
            for c in range(1, 5):
                tile(0, c)
            pipelined(pe, 5, NT - 3, tile, 4)
            tile(0, NT - 2)
            tile(0, NT - 1, t=False)
            tile(0, NT, t=False, u=False)

        @block.scalar
        def _(act):
            act.wait_ge(S["wq_in"], 16)
            act.activation(wq_stage, wq_stage, ACT.Copy, scale=SW).then_inc(S["split_high"], 1)
            act.wait_ge(S["split_high"], 1)
            act.activation(wp[:, 0].rearrange("p q k d -> p (q k d)"), wq_stage, ACT.Copy).then_inc(S["split_high"], 1)

            def split_weights(b, q, slot):
                m = b.n * CPS + q
                act.wait_ge(st_in[slot], (CPS * b.j + (CPS * b.c + q) // 2) * 16 + 16)
                act.activation(wst[:, slot], wst[:, slot], ACT.Copy, scale=SW).then_inc(S["we_scaled"], 1)
                act.wait_ge(S["we_scaled"], m + 1)
                act.activation(wes[:, 0, bass.ds(m * WCH, WCH)], wst[:, slot], ACT.Copy).then_inc(S["we_high"], 1)

            def high(a):
                wait(act, "xn_ready", a.upto(C))
                wait(act, "t1_done", a.upto(2, -1))
                act.activation(xhl[:, 0], xs[:, a.par], ACT.Copy).then_inc(S["xh_ready"], 1)

            def one(j, c):
                n, p, m, r = stages(c)
                a1, a, b, z = (Seq(j, c + 2 - q) for q in range(4))
                slot = lambda q: (CPS * c + q) % 2
                if r:
                    for k in range(KD):
                        act.wait_ge(S["x2t_done"], z.upto(KD, k + 1))
                        wait(act, "lg_done", z.upto(1, 0))
                        act.activation(x2T[:, k], bank(k), ACT.Copy).then_inc(S["x2T_ready"], 1)
                if p:
                    for h in range(NH):
                        act.wait_ge(S["kp_done"], a.upto(NH, h + 1))
                        if h == 0:
                            wait(act, "kt_ready", a.upto(1, 0))
                        act.activation(ff[:, h * L:(h + 1) * L], bank(2 + h), ACT.Sigmoid, scale=1 / (SX * SW)).then_inc(S["sig_k"], 1)
                        wait(act, "kt_done", a.upto(NH, 0))
                        act.activation(kk[:, h], bank(2 + h), ACT.Sigmoid, scale=-1 / (SX * SW)).then_inc(S["sig_k"], 1)
                    act.wait_ge(S["sig_k"], a.upto(2 * NH))
                    act.activation(ff[:], ff[:], ACT.Sigmoid).then_inc(S["dec_ready"], 1)
                if m:
                    split_weights(b, 0, slot(0))
                    sq = xs[:, 1 - b.par].rearrange("p c d -> p (c d)")
                    for h in range(NH):
                        act.wait_ge(S["ot_done"], b.upto(NH, h + 1))
                        wait(act, "y_done", b.upto(2, 0))
                        act.activation(ots[:, h], bank(6 + h), ACT.Copy).then_inc(S["ots_ready"], 1)
                        act.activation(sq[:, h * L:(h + 1) * L], bank(6 + h), ACT.Square).then_inc(S["sq_ready"], 1)
                if r:
                    act.wait_ge(S["route_a"], z.upto(ROUTE_A))
                    for i, sign in enumerate((1, -1)):
                        act.activation(wsig[:, i], rc[:, 6], ACT.Sigmoid, scale=sign / SX).then_inc(S["wsig_ready"], 1)
                if p:
                    for h in range(NH):
                        act.wait_ge(S["qp_done"], a.upto(NH, h + 1))
                        wait(act, "qt_ready", a.upto(1, 0))
                        act.activation(qq[:, h], bank(2 + h), ACT.Sigmoid, scale=1 / (SX * SW)).then_inc(S["sig_q"], 1)
                if m:
                    for q in range(1, CPS):
                        split_weights(b, q, slot(q))
                if p:
                    for pair in range(2):
                        act.wait_ge(S["vp_done"], a.upto(2, pair + 1))
                        act.activation(vv[:, a.par, 2 * pair:2 * pair + 2].rearrange("p c d -> p (c d)"), bank(2 + pair), ACT.Copy,
                                       scale=1 / (SX * SW)).then_inc(S["v_ready"], 1)
                if n:
                    wait(act, "xn_ready", a1.upto(C))
                    wait(act, "t1_done", a1.upto(2, -1))
                    act.activation(xhl[:, 0], xs[:, a1.par], ACT.Copy).then_inc(S["xh_ready"], 1)
                if p:
                    for h in range(NH):
                        wait(act, "kt_done", a.upto(NH, h + 1))
                        act.activation(kTs[:, h], bank(6 + h)[:, 0:(C - 1) * P].rearrange("p (c t) -> p c t", t=P),
                                       ACT.Copy).then_inc(S["kts_ready"], 1)
                if n:
                    for part in range(2):
                        wait(act, "t1_done", a1.upto(2, part + 1))
                        wait(act, "vp_done", a1.upto(2, 0))
                        act.activation(xT[:, part], bank16(part).rearrange("p (k t) -> p k t", t=L), ACT.Copy)\
                            .then_inc(S["xT_ready"], 1)
                if m:
                    act.wait_ge(S["xn2_ready"], b.upto(C))
                    wait(act, disp[b.par], b.half * (2 * C * 16))
                    act.activation(rows[:, b.par, :, 0:D], xn2[:], ACT.Copy).then_inc(S["rowhi_ready"], 1)

            act.wait_ge(S["setup"], SETUP)
            for c in range(-2, 3):
                one(0, c)
            pipelined(act, 3, 4, one)
            for c in range(5, NSEQ + 1):
                one(0, c)

            def tile(j, c, t=True, u=True):
                i = Tile(j, c)
                if t:
                    a = Tile(j, c + 1)
                    act.wait_ge(S["tx_done"], a.upto(1))
                    wait(act, "g1_done", a.upto(FJ, -FJ))
                    act.activation(xTm(a), bank16(4 + a.par).rearrange("p (q t) -> p q t", t=RT), ACT.Copy).then_inc(S["xtc_ready"], 1)
                if u:
                    e = act.value_load(etab[0:1, bass.ds(i.n, 1)], min_val=0, max_val=E - 1)
                    wait(act, "h_ready", i.upto(4, -4))
                    for q in range(FJ):
                        act.wait_ge(S["g1_done"], i.upto(FJ, q + 1))
                        act.activation(silu_of(i)[:, q, :], bank(q)[:, 0:RT], ACT.Silu, bias=b1s[:, bass.ds(e * 2 * FJ + q, 1)],
                                       scale=ALPHA / (SX * SW)).then_inc(S["sv_ready"], 1)
                        act.activation(value_of(i)[:, q, :], bank(q)[:, RT:2 * RT], ACT.Identity,
                                       bias=b1s[:, bass.ds(e * 2 * FJ + (FJ + q), 1)],
                                       scale=SH / (ALPHA * SX * SW)).then_inc(S["sv_ready"], 1)

            tile(0, -1, u=False)
            tile(0, 0)
            for c in range(1, 5):
                tile(0, c)
            pipelined(act, 5, NT - 3, tile, 4)
            tile(0, NT - 2)
            tile(0, NT - 1, t=False)

        @block.vector
        def _(dve):
            def row_stats(b, src, st_, mv_, stats_sem, mv_sem):
                for c in range(C):
                    dve.bn_stats(st_[:, c, :], src[:, c, :]).then_inc(S[stats_sem], 1)
                wait_apart(dve, (S[stats_sem], b.upto(C)))
                for c in range(C):
                    dve.bn_aggr(mv_[:, c, :], st_[:, c, :]).then_inc(S[mv_sem], 1)

            def stats1(a):
                dve.wait_ge(x_in[a.par], a.upto_half(16))
                row_stats(a, xs[:, a.par], st, mv1, "ln1_stats", "ln1_mv")

            def normalise1(a):
                dve.wait_ge(S["rstd1"], a.upto(1))
                for c in range(C):
                    dve.tensor_scalar(xs[:, a.par, c], xs[:, a.par, c], mv1[:, c, 0:1], rs1[:, c:c + 1], ALU.subtract, ALU.mult)\
                        .then_inc(S["xn_ready"], 1)

            def low1(a):
                dve.wait_ge(S["xh_ready"], a.upto(1))
                wait(dve, "t1_done", a.upto(2, 0))
                dve.tensor_tensor(xhl[:, 1], xs[:, a.par], xhl[:, 0], ALU.subtract).then_inc(S["xl_ready"], 1)

            def decays(a):
                d = ff[:].rearrange("p (g s t) -> p g s t", s=2, t=HALF)
                starts = ff[:].rearrange("p (g t) -> p g t", t=HALF)[:, :, 0]
                dve.wait_ge(S["dec_ready"], a.upto(1))
                dve.tensor_copy(resets[:].rearrange("p (g t) -> p g t", t=HALF)[:, :, 0], starts).then_inc(S["scan_prep"], 1)
                dve.wait_ge(S["scan_prep"], a.upto(2, 1))
                dve.memset(starts, 0.0).then_inc(S["scan_prep"], 1)
                dve.wait_ge(S["scan_prep"], a.upto(2))
                dve.tensor_tensor_scan(ff[:], ff[:], resets[:], 0.0, ALU.mult, ALU.add).then_inc(S["scan_done"], 1)
                dve.wait_ge(S["scan_done"], a.upto(1))
                dve.tensor_copy(dmid[:], d[:, :, 0, HALF - 1]).then_inc(S["mid_done"], 1)
                dve.tensor_copy(dend[:], d[:, :, 1, HALF - 1]).then_inc(S["mid_done"], 1)
                dve.wait_ge(S["mid_done"], a.upto(3, 2))
                dve.reciprocal(rmid[:], dmid[:]).then_inc(S["rmid_done"], 1)
                dv, mv = dend[:].rearrange("p (h c) -> p h c", c=C), dmid[:].rearrange("p (h c) -> p h c", c=C)
                dve.tensor_tensor(gg[:], dv[:, :, 0:C - 1], mv[:, :, 1:C], ALU.mult).then_inc(S["mid_done"], 1)
                dve.wait_ge(S["rmid_done"], a.upto(1))
                dve.tensor_tensor(d[:, :, 0, :], d[:, :, 0, :], rmid[:].unsqueeze(2).broadcast_to((P, NH * C, HALF)), ALU.mult)\
                    .then_inc(S["e_done"], 1)

            def keys_queries(a):
                for h in range(NH):
                    dve.wait_ge(S["sig_q"], a.upto(NH, h + 1))
                    dve.scalar_tensor_tensor(out=qq[:, h], in0=bank(2 + h), scalar=1 / (SX * SW), in1=qq[:, h],
                                             op0=ALU.mult, op1=ALU.mult).then_inc(S["q_done"], 1)
                dve.wait_ge(S["q_done"], a.upto(NH))
                dve.wait_ge(S["e_done"], a.upto(1))
                dve.tensor_tensor(flat(qt)[:, a.par * NH * L:(a.par + 1) * NH * L], flat(qq), ff[:], ALU.mult).then_inc(S["qt_ready"], 1)
                dve.wait_ge(S["qt_ready"], a.upto(1))
                dve.reciprocal(ff[:], ff[:]).then_inc(S["re_done"], 1)
                dve.wait_ge(S["re_done"], a.upto(1))
                dve.tensor_tensor(flat(kk), flat(kk), ff[:], ALU.mult).then_inc(S["kt_ready"], 1)

            def masks(b):
                wait(dve, "ot_done", b.upto(NH, 0))
                m = const("mask")
                for h in range(NH):
                    dve.wait_ge(S["a_done"], b.upto(NH, h + 1))
                    sc = bank(4 + h).rearrange("p (c t) -> p c t", t=P)
                    dve.tensor_tensor(at[0:HALF, h], sc[0:HALF], m[0:HALF].unsqueeze(1).broadcast_to((HALF, C, P)), ALU.mult)\
                        .then_inc(S["at_ready"], 1)
                    dve.tensor_tensor(at[HALF:P, h, :, HALF:P], sc[HALF:P, :, HALF:P],
                                      m[HALF:P, HALF:P].unsqueeze(1).broadcast_to((HALF, C, HALF)), ALU.mult).then_inc(S["at_ready"], 1)

            def states(b):
                dve.wait_ge(S["kv_done"], b.upto(1))
                kv = ps[:, 4:4 + NH, :]
                g = lambda c: gg[:, :, c:c + 1].broadcast_to((P, NH, P))
                dve.tensor_tensor(sm[:, 0], kv[:, :, 0:P], g(0), ALU.mult).then_inc(S["sm_ready"], 1)
                for c in (1, 2):
                    dve.wait_ge(S["sm_ready"], b.upto(5, 2 * c - 1))
                    dve.tensor_tensor(smt[:], kv[:, :, c * P:(c + 1) * P], sm[:, c - 1], ALU.add).then_inc(S["sm_ready"], 1)
                    dve.wait_ge(S["sm_ready"], b.upto(5, 2 * c))
                    dve.tensor_tensor(sm[:, c], smt[:], g(c), ALU.mult).then_inc(S["sm_ready"], 1)

            def over_experts(v):
                return v.unsqueeze(2).broadcast_to((P, C, E))

            def over_tokens(v):
                return v.unsqueeze(1).broadcast_to((P, C, E))

            def chain(name, z, per):
                k = [0]

                def step(ins, hold=True):
                    ins.then_inc(S[name], 1)
                    k[0] += 1
                    if hold:
                        dve.wait_ge(S[name], z.upto(per, k[0]) if z else k[0])
                    return k[0]
                return step, k

            def route_a(z):
                dve.wait_ge(S["lg_done"], z.upto(1))
                step, k = chain("route_a", z, ROUTE_A)
                logits = bank(5)[:, 0:C * E].rearrange("p (c e) -> p c e", e=E)
                for n, src in ((0, logits), (1, rt[:, 2])):
                    step(dve.tensor_reduce(rc[:, 2 * n], src, AX, ALU.max))
                    step(dve.tensor_tensor(rt[:, 0], src, over_experts(rc[:, 2 * n]), ALU.is_equal))
                    step(dve.tensor_tensor(rt[:, 0], rt[:, 0], over_tokens(const("tie")), ALU.mult))
                    step(dve.tensor_reduce(rc[:, 2 * n + 1], rt[:, 0], AX, ALU.max))
                    step(dve.tensor_tensor(rt[:, 1 + 2 * n], rt[:, 0], over_experts(rc[:, 2 * n + 1]), ALU.is_equal))
                    if n == 0:
                        step(dve.scalar_tensor_tensor(out=rt[:, 2], in0=rt[:, 1], scalar=-3e38, in1=logits, op0=ALU.mult, op1=ALU.add))
                step(dve.tensor_tensor(rc[:, 6], rc[:, 0], rc[:, 2], ALU.subtract), hold=False)
                step(dve.tensor_tensor(msel[:], rt[:, 1], rt[:, 3], ALU.add), hold=False)
                assert k[0] == ROUTE_A

            def route_b(z):
                dve.wait_ge(S["rk_done"], z.upto(1))
                step, k = chain("route_b", z, ROUTE_B)
                rank = bank(5)[:, 64:64 + C * E].rearrange("p (c e) -> p c e", e=E)
                step(dve.tensor_tensor(rt[:, 4], rank, over_tokens(cnt[:]), ALU.add))
                step(dve.tensor_tensor(cnt[:], cnt[:], bank(5)[:, 128:128 + E], ALU.add))
                for n in range(2):
                    step(dve.tensor_tensor(rt[:, 5], rt[:, 4], rt[:, 1 + 2 * n], ALU.mult))
                    step(dve.tensor_reduce(rc[:, 4 + n], rt[:, 5], AX, ALU.add))
                step(dve.tensor_copy(dest[:, z.par], rc[:, 4:6]), hold=False)
                dve.wait_ge(S["wsig_ready"], z.upto(2))
                words = rows32[:, z.par]
                step(dve.tensor_scalar(words[:, :, D + 3], rc[:, 1], -1.0, float(E), ALU.mult, ALU.add), hold=False)
                step(dve.tensor_scalar(words[:, :, D + 1], wsig[:, 1], 1 / (SH * SW), None, ALU.mult))
                step(dve.scalar_tensor_tensor(out=words[:, :, D + 2], in0=wsig[:, 0], scalar=1 / (SH * SW), in1=words[:, :, D + 1],
                                              op0=ALU.mult, op1=ALU.subtract), hold=False)
                assert k[0] == ROUTE_B

            def residual(b):
                dve.wait_ge(S["rms_ready"], b.upto(1))
                dve.wait_ge(S["xr_in"], b.upto(16))
                for c in range(C):
                    if c % 2 == 0:
                        dve.wait_ge(S["y_done"], b.upto(2, c // 2 + 1))
                    dve.scalar_tensor_tensor(out=xr[:, c], in0=bank(c // 2)[:, c % 2 * D:(c % 2 + 1) * D], scalar=rms[:, c:c + 1],
                                             in1=xr[:, c], op0=ALU.mult, op1=ALU.add).then_inc(S["x2_ready"], 1)

            def normalise2(b):
                dve.wait_ge(S["rstd2"], b.upto(1))
                wait(dve, "x2t_done", b.upto(KD, 0))
                wait(dve, "rowlo_ready", b.upto(1, 0))
                for c in range(C):
                    dve.tensor_scalar(xn2[:, c], xr[:, c], mv2[:, c, 0:1], rs2[:, c:c + 1], ALU.subtract, ALU.mult)\
                        .then_inc(S["xn2_ready"], 1)

            def one(j, c):
                n, p, m, r = stages(c)
                a1, a, b, z = (Seq(j, c + 2 - q) for q in range(4))
                if m:
                    states(b)
                if n:
                    stats1(a1)
                if r:
                    route_a(z)
                if p:
                    decays(a)
                if r:
                    route_b(z)
                if m:
                    dve.wait_ge(S["ss_done"], b.upto(1))
                    dve.tensor_scalar(ssv[:], bank(4)[:, 0:C], 1 / D, EPS_RMS, ALU.mult, ALU.add).then_inc(S["ssv_ready"], 1)
                if p:
                    keys_queries(a)
                if n:
                    normalise1(a1)
                if m:
                    residual(b)
                if p:
                    masks(a)
                if m:
                    dve.wait_ge(S["x2_ready"], b.upto(C))
                    row_stats(b, xr, st2, mv2, "ln2_stats", "ln2_mv")
                if n:
                    low1(a1)
                if m:
                    normalise2(b)

            step, k = chain("setup", None, 0)
            step(dve.memset(resets[:], 0.0), hold=False)
            step(dve.memset(at[HALF:P, :, :, 0:HALF], 0.0), hold=False)
            step(dve.memset(ones2[:], SW), hold=False)
            dve.wait_ge(S["const_in"], 32)
            dve.wait_ge(S["small_in"], 64)
            dve.wait_ge(S["wo_in"], 32)
            step(dve.tensor_copy(cnt[:], const("base")), hold=False)
            for h in range(NH):
                step(dve.tensor_scalar(wos[:, h], wos[:, h], nws[:, h:h + 1], None, ALU.mult), hold=False)
            b1v = b1s[:].rearrange("p (e g j) -> p e g j", g=2, j=FJ)
            step(dve.tensor_scalar(b1v[:, :, 0], b1v[:, :, 0], ALPHA, None, ALU.mult), hold=False)
            step(dve.tensor_scalar(b1v[:, :, 1], b1v[:, :, 1], 1.0, SH / ALPHA, ALU.add, ALU.mult), hold=False)
            b2v = flat(vv)[0:2, :]
            step(dve.tensor_scalar(b2v, b2v, SH, None, ALU.mult))
            step(dve.tensor_copy(b2s[:], b2v))
            step(dve.scalar_tensor_tensor(out=b2s[:], in0=b2s[:], scalar=cfs[0:2, CF["low"][0]:CF["low"][1]], in1=b2v,
                                          op0=ALU.mult, op1=ALU.add), hold=False)
            dve.wait_ge(S["zero_out"], 16)
            step(dve.memset(resets[:, 0:1], 0.0), hold=False)
            assert k[0] == SETUP
            dve.wait_ge(S["split_high"], 2)
            dve.tensor_tensor(wp[:, 1].rearrange("p q k d -> p (q k d)"), wq_stage, wp[:, 0].rearrange("p q k d -> p (q k d)"),
                              ALU.subtract).then_inc(S["split_low"], 1)

            iterations(dve, one)

            step, k = chain("plan_done", None, 0)
            ptile = flat(x2T)[:, 0:3 * NT * E].rearrange("p (a t e) -> p a t e", a=3, e=E)
            cols = lambda v: v.unsqueeze(1).broadcast_to((P, NT, E))
            tiles = lambda v: v.unsqueeze(2).broadcast_to((P, NT, E))
            step(dve.tensor_copy(plani[:, 2], cnt[:]))
            step(dve.tensor_tensor(plan[:, 0], cnt[:], const("base"), ALU.subtract))
            step(dve.tensor_scalar(plani[:, 0], plan[:, 0], float(RT - 1), None, ALU.add))
            step(dve.tensor_scalar(plani[:, 1], plani[:, 0], RT.bit_length() - 1, None, ALU.logical_shift_right))
            step(dve.tensor_copy(plan[:, 0], plani[:, 1]))
            step(dve.tensor_tensor_scan(plan[:, 1], const("ones"), plan[:, 0], 0.0, ALU.mult, ALU.add))
            step(dve.tensor_tensor(plan[:, 2], plan[:, 1], plan[:, 0], ALU.subtract))
            step(dve.scalar_tensor_tensor(out=plan[:, 3], in0=plan[:, 2], scalar=-float(RT), in1=const("base"),
                                          op0=ALU.mult, op1=ALU.add))
            step(dve.tensor_tensor(ptile[:, 0], cols(plan[:, 1]), tiles(const("tile")), ALU.is_le))
            step(dve.tensor_reduce(pt[:, 0], ptile[:, 0], AX, ALU.add))
            step(dve.tensor_tensor(ptile[:, 1], tiles(pt[:, 0]), cols(const("eidx")), ALU.is_equal))
            step(dve.tensor_tensor(ptile[:, 2], ptile[:, 1], cols(plan[:, 3]), ALU.mult))
            step(dve.tensor_reduce(pt[:, 1], ptile[:, 2], AX, ALU.add))
            step(dve.tensor_scalar(pt[:, 2], pt[:, 0], float(E), None, ALU.is_lt))
            step(dve.tensor_tensor(pt[:, 3], pt[:, 2], const("tile_row"), ALU.mult))
            step(dve.tensor_tensor(pt[:, 1], pt[:, 1], pt[:, 3], ALU.add))
            step(dve.tensor_scalar(roff[:], pt[:, 1], float(SPARE), None, ALU.add), hold=False)
            step(dve.tensor_scalar(etab[:], pt[:, 0], float(E - 1), None, ALU.min), hold=False)
            assert k[0] == PLAN

            def tile(j, c, u=True, d=True):
                i, z = Tile(j, c), Tile(j, c - 1)
                if u:
                    h = flat(xs)[:, 0:FJ * RT]
                    v, g = (t(i).rearrange("p q t -> p (q t)") for t in (value_of, silu_of))
                    hi, lo = (hhl(i)[:, n].rearrange("p q t -> p (q t)") for n in range(2))
                    dve.wait_ge(S["sv_ready"], i.upto(2 * FJ))
                    dve.tensor_scalar(v, v, (LIMIT + 1) * SH / ALPHA, (1 - LIMIT) * SH / ALPHA, ALU.min, ALU.max).then_inc(S["h_ready"], 1)
                    dve.wait_ge(S["h_ready"], i.upto(4, 1))
                    dve.scalar_tensor_tensor(out=h, in0=g, scalar=SILU_MAX, in1=v, op0=ALU.min, op1=ALU.mult).then_inc(S["h_ready"], 1)
                    dve.wait_ge(S["h_ready"], i.upto(4, 2))
                    wait(dve, "g2_done", i.upto(1, -1))
                    dve.tensor_copy(hi, h).then_inc(S["h_ready"], 1)
                    dve.wait_ge(S["h_ready"], i.upto(4, 3))
                    dve.tensor_tensor(lo, h, hi, ALU.subtract).then_inc(S["h_ready"], 1)
                if d:
                    dve.wait_ge(S["g2_done"], z.upto(1))
                    dve.wait_ge(S["w_ready"], z.upto(WSTEPS))
                    wait(dve, "added", z.upto(32, -32))
                    for s in range(SR):
                        dve.tensor_scalar(y_of(z)[:, s], bank(6 + z.par)[:, s * D:(s + 1) * D], wrow[:, z.slot, 1, s:s + 1], None,
                                          ALU.mult).then_inc(S["y_ready"], 1)

            tile(0, 0, d=False)
            for c in range(1, 5):
                tile(0, c)
            pipelined(dve, 5, NT - 3, tile, 4)
            tile(0, NT - 2)
            tile(0, NT - 1)
            tile(0, NT, u=False)

        @block.gpsimd
        def _(pool):
            pool.wait_ge(S["const_in"], 32)

            def rstd(b, mv_, var_sem, out_, out_sem, mv_sem):
                wait_apart(pool, (S[mv_sem], b.upto(C)))
                pool.tensor_scalar(pw[:, 0], mv_[:, :, 1], EPS_LN, None, ALU.add).then_inc(S[var_sem], 1)
                pool.wait_ge(S[var_sem], b.upto(2, 1))
                pool.tensor_tensor(pw[:, 1], pw[:, 0], const("half"), ALU.pow).then_inc(S[var_sem], 1)
                wait_apart(pool, (S[var_sem], b.upto(2)))
                pool.tensor_scalar(out_[:], pw[:, 1], SX, None, ALU.mult).then_inc(S[out_sem], 1)

            def one(j, c):
                n, p, m, r = stages(c)
                a1, b, z = Seq(j, c + 2), Seq(j, c), Seq(j, c - 1)
                if r:
                    wait_apart(pool, ("rowhi_ready", z.upto(1)))
                    pool.tensor_tensor(rows[:, z.par, :, D:2 * D], xn2[:], rows[:, z.par, :, 0:D], ALU.subtract).then_inc(S["rowlo_ready"], 1)
                    at_ = CF["tok"][0]
                    pool.tensor_copy(rows_i[:, z.par, :, D], cfs[:].bitcast(I32)[:, bass.ds(z.n * C + at_, C)]).then_inc(S["tok_ready"], 1)
                if n:
                    rstd(a1, mv1, "ln1_var", rs1, "rstd1", "ln1_mv")

                def low_parts(q):
                    m, slot = b.n * CPS + q, (CPS * c + q) % 2
                    pool.wait_ge(S["we_high"], m + 1)
                    pool.tensor_tensor(wes[:, 1, bass.ds(m * WCH, WCH)], wst[:, slot], wes[:, 0, bass.ds(m * WCH, WCH)],
                                       ALU.subtract).then_inc(S["we_low"], 1)

                if m:
                    low_parts(0)
                if r:
                    wait_apart(pool, ("route_b", z.upto(ROUTE_B)), ("rowlo_ready", z.upto(1)), ("tok_ready", z.upto(1)))
                    for c_ in range(C):
                        for i in range(2):
                            pool.indirect_dma_start(rows_dram, bass.IndirectOffsetOnAxis(ap=dest[:, z.par, i, c_:c_ + 1], axis=0),
                                                    rows_i[:, z.par, c_, :], None).then_inc(disp[z.par], 16)
                if m:
                    pool.wait_ge(S["ssv_ready"], b.upto(1))
                    pool.tensor_tensor(rms[:], ssv[:], const("half"), ALU.pow).then_inc(S["rms_ready"], 1)
                    for q in range(1, CPS):
                        low_parts(q)
                    rstd(b, mv2, "ln2_var", rs2, "rstd2", "ln2_mv")
            iterations(pool, one)

            pool.wait_ge(S["plan_done"], PLAN)
            pool.wait_ge(S["x2_out"], 16 * NSEQ)
            pool.wait_ge(S["zero_out"], 16)

            def tile(j, c, u=True, d=True):
                i, z = Tile(j, c), Tile(j, c - 1)
                if u:
                    wait_apart(pool, (xg_in[i.slot], i.turn * 16 + 16),
                                     ("added", i.upto(32, -96)))
                    m = meta[:, i.slot]
                    pool.tensor_copy(token[:, i.slot], row_buffer(rows_i, i)[:, :, D]).then_inc(S["meta_ready"], 1)
                    pool.tensor_copy(m, row_buffer(rows32, i)[:, :, D + 1:D + 4]).then_inc(S["meta_ready"], 1)
                    pool.wait_ge(S["meta_ready"], i.upto(2))
                    ef = pt[:, 0, bass.ds(i.n, 1)].broadcast_to((P, SR))
                    same, w = wrow[:, i.slot, 0], wrow[:, i.slot, 1]
                    pool.tensor_tensor(same, m[:, :, 2], ef, ALU.subtract).then_inc(S["w_ready"], 1)
                    wait_apart(pool, ("w_ready", i.upto(WSTEPS, 1)))
                    pool.tensor_scalar(same, same, 0.0, None, ALU.is_equal).then_inc(S["w_ready"], 1)
                    pool.wait_ge(S["w_ready"], i.upto(WSTEPS, 2))
                    pool.tensor_tensor(w, same, m[:, :, 1], ALU.mult).then_inc(S["w_ready"], 1)
                    pool.wait_ge(S["w_ready"], i.upto(WSTEPS, 3))
                    pool.tensor_tensor(w, w, m[:, :, 0], ALU.add).then_inc(S["w_ready"], 1)
                if d:
                    wait_apart(pool, ("y_ready", z.upto(SR)),
                                     ("added", z.upto(32, 0)))
                    for s in range(SR):
                        pool.indirect_dma_start(out, bass.IndirectOffsetOnAxis(ap=token[:, z.slot, s:s + 1], axis=0),
                                                y_of(z)[:, s], None, compute_op=ALU.add).then_inc(S["added"], 16)

            tile(0, 0, d=False)
            for c in range(1, 5):
                tile(0, c)
            pipelined(pool, 5, NT - 3, tile, 4)
            tile(0, NT - 2)
            tile(0, NT - 1)
            tile(0, NT, u=False)


def constants():
    import numpy as np

    cf = np.zeros((P, CFN), np.float32)
    p = np.arange(P)

    def put(name, v):
        a, b = CF[name]
        cf[:, a:b] = v

    put("ident", np.eye(P))
    put("mask", p[:, None] <= p[None, :])
    put("base", np.arange(E) * REGION)
    put("tie", E - np.arange(E))
    put("eidx", np.arange(E))
    put("tile", np.arange(NT))
    put("tile_row", np.arange(NT) * RT - SPARE)
    put("half", -0.5)
    put("ones", 1.0)
    put("low", -1.0 * (p[:, None] == 1))
    a, b = CF["tok"]
    cf[:, a:b].view(np.int32)[:] = np.arange(T // P)[None, :] * P + p[:, None]
    ch = np.concatenate([np.eye(P), p[:, None] < p[None, :], np.ones((P, P))], 1).astype(np.float16)
    words = np.zeros((P, SR, WORDS), np.int32)
    words[:, :, D] = T + np.arange(SR)[None, :] * P + p[:, None]
    words[:, :, D + 3] = np.float32(-1.0).view(np.int32)
    return cf, ch, words


def kernel(L0_attn_x, L0_attn_Wq, L0_attn_Wk, L0_attn_Wv, L0_attn_Wo, L0_attn_norm_w, L0_ffn_gate_w,
           L0_ffn_dense_1_w, L0_ffn_dense_1_b, L0_ffn_dense_2_w, L0_ffn_dense_2_b):
    import numpy as np
    import concourse.bacc as bacc
    from concourse.bass_utils import run_bass_kernel_spmd

    def halves(w):
        return np.asarray(w).T.reshape(KD, P, D).transpose(1, 0, 2)

    x = np.ascontiguousarray(np.asarray(L0_attn_x).reshape(T, D))
    wqkv = np.stack([halves(w) for w in (L0_attn_Wq, L0_attn_Wk, L0_attn_Wv)], 1).reshape(P, 3 * KD * D)
    wo = np.ascontiguousarray(halves(L0_attn_Wo))
    norm_w = np.ascontiguousarray(np.asarray(L0_attn_norm_w).reshape(NH, P).T)
    gate_w = np.ascontiguousarray(np.asarray(L0_ffn_gate_w).reshape(KD, P, E).transpose(1, 0, 2))
    w1 = np.asarray(L0_ffn_dense_1_w).reshape(E, FF, 2, KD, P).transpose(4, 0, 3, 2, 1).reshape(P, W1COLS)
    w2 = np.asarray(L0_ffn_dense_2_w).reshape(E, D, FJ, P).transpose(3, 0, 2, 1).reshape(P, W2COLS)
    we = np.concatenate([w1, w2], 1)
    b1 = np.ascontiguousarray(np.asarray(L0_ffn_dense_1_b).reshape(E, FJ, P, 2).transpose(2, 0, 3, 1).reshape(P, E * 2 * FJ))
    b2 = np.ascontiguousarray(np.asarray(L0_ffn_dense_2_b).reshape(1, E * D))
    cf, ch, pad = constants()
    arrays = dict(x=x, wqkv=wqkv, wo=wo, norm_w=norm_w, gate_w=gate_w, we=we, b1=b1, b2=b2, cf=cf, ch=ch, pad=pad)

    nc = bacc.Bacc("TRN2", target_bir_lowering=False, num_devices=1)
    args = [nc.dram_tensor(n, a.shape, mybir.dt.from_np(a.dtype), kind="ExternalInput").ap() for n, a in arrays.items()]
    args.append(nc.dram_tensor("out", (T + RT, D), F32, kind="ExternalOutput").ap())
    build_kernel(nc, *args)
    got = run_bass_kernel_spmd(nc, [arrays], core_ids=[0]).results[0]["out"]
    return got[0:T].reshape(NSEQ, L, D)
```

```python
import math
from contextlib import ExitStack

import concourse.bass as bass
from concourse import mybir

ALU = mybir.AluOpType
ACT = mybir.ActivationFunctionType
AX = mybir.AxisListType.X
F32 = mybir.dt.float32
F16 = mybir.dt.float16
I32 = mybir.dt.int32
U32 = mybir.dt.uint32

P = 128
NSEQ, L, D = 8, 512, 256
T = NSEQ * L
C = L // P
KD = D // P
NH = KD
HALF = P // 2
E, FF = 8, 512
FJ = FF // P
RT = 256
SR = RT // P
REGION = T + RT
SPARE = E * REGION
NT = 2 * T // RT + E - 1
ROW = 2 * D + 8
WORDS = ROW // 2

SX = 2.0 ** 11
SW = 2.0 ** 8
SH = 2.0 ** 8
ALPHA, LIMIT = 1.702, 9.0
SILU_MAX = ALPHA * LIMIT / (1 + math.exp(-ALPHA * LIMIT))
EPS_LN, EPS_RMS = 1e-5, 1e-6
WCH = 1024
W1COLS, W2COLS = E * KD * 2 * FF, E * FJ * D
NCH = (W1COLS + W2COLS) // WCH
CPS = NCH // NSEQ
SETUP, ROUTE_A, ROUTE_B, PLAN, WSTEPS = 12, 12, 8, 18, 4

CF = {}
_at = 0
for _name, _n in (("ident", P), ("mask", P), ("base", E), ("eidx", E), ("tile", NT), ("tile_row", NT),
                  ("half", C), ("ones", E), ("low", 1), ("tok", T // P)):
    CF[_name] = (_at, _at + _n)
    _at += _n
CFN = _at


class Seq:

    def __init__(self, j, c, unroll=2):
        self.j, self.c = j, c
        self.n = unroll * j + c
        self.par = c % 2
        self.half = unroll // 2 * j + c // 2

    def upto(self, per, count=None):
        return self.n * per + (per if count is None else count)

    def upto_half(self, per):
        return self.half * per + per


class Tile(Seq):

    def __init__(self, j, c):
        super().__init__(j, c, 4)
        self.slot = c % 4
        self.turn = j + c // 4


def build_kernel(nc, x, wqkv, wo, norm_w, gate_w, we, b1, b2, cf, ch, pad, out):
    rows_dram = nc.dram_tensor("dispatched_rows", (SPARE + REGION, WORDS), I32).ap()

    with ExitStack() as ctx:
        def sb(name, shape, dt=F32):
            return ctx.enter_context(nc.sbuf_tensor(name, shape, dt))

        def sem(name):
            return ctx.enter_context(nc.semaphore(name))

        wes = sb("wes", [P, 2, W1COLS + W2COLS], F16)
        wst = sb("wst", [P, 2, WCH])
        wp = sb("wp", [P, 2, 3, KD, D], F16)
        wos = sb("wos", [P, NH, D])
        nws = sb("nws", [P, NH])
        gws = sb("gws", [P, KD, E])
        b1s = sb("b1s", [P, E * 2 * FJ])
        b2s = sb("b2s", [2, E * D], F16)
        ones2 = sb("ones2", [2, P], F16)
        cfs = sb("cfs", [P, CFN])
        chs = sb("chs", [P, 3 * P], F16)
        xs = sb("xs", [P, 2, C, D])
        xr = sb("xr", [P, C, D])
        xhl = sb("xhl", [P, 2, C, D], F16)
        xT = sb("xT", [P, 2, KD, L], F16)
        ff = sb("ff", [P, NH * L])
        kk = sb("kk", [P, NH, L])
        qq = sb("qq", [P, NH, L])
        resets = sb("resets", [P, NH * L])
        qt = sb("qt", [P, 2, NH, L])
        vv = sb("vv", [P, 2, C, D])
        at = sb("at", [P, NH, C, P])
        kTs = sb("kTs", [P, NH, C - 1, P])
        sm = sb("sm", [P, C - 1, NH, P])
        smt = sb("smt", [P, NH, P])
        ots = sb("ots", [P, NH, L])
        xn2 = sb("xn2", [P, C, D])
        x2T = sb("x2T", [P, KD, L])
        rows = sb("rows", [P, 2, C, ROW], F16)
        st = sb("st", [P, C, 6])
        st2 = sb("st2", [P, C, 6])
        mv1 = sb("mv1", [P, C, 2])
        mv2 = sb("mv2", [P, C, 2])
        pw = sb("pw", [P, 4, C])
        rs1 = sb("rs1", [P, C])
        rms = sb("rms", [P, C])
        rs2 = sb("rs2", [P, C])
        ssv = sb("ssv", [P, C])
        dmid = sb("dmid", [P, NH * C])
        dend = sb("dend", [P, NH * C])
        rmid = sb("rmid", [P, NH * C])
        gg = sb("gg", [P, NH, C - 1])
        lmax = sb("lmax", [P, C, E])
        lidx = sb("lidx", [P, C, E], U32)
        chosen = sb("chosen", [P, 2, C])
        onehot = sb("onehot", [P, 2, C, E])
        places = sb("places", [P, C, E])
        picked = sb("picked", [P, 2, C, E])
        place = sb("place", [P, 2, C])
        gap = sb("gap", [P, C])
        msel = sb("msel", [P, C, E], F16)
        wsig = sb("wsig", [P, 2, C])
        cnt = sb("cnt", [P, E])
        dest = sb("dest", [P, 2, 2, C], I32)
        plan = sb("plan", [P, 4, E])
        plani = sb("plani", [P, 3, E], I32)
        pt = sb("pt", [P, 4, NT])
        roff = sb("roff", [P, NT], I32)
        etab = sb("etab", [P, NT], I32)
        pads = sb("pads", [P, SR, WORDS], I32)
        meta = sb("meta", [P, 4, SR, 3])
        token = sb("token", [P, 4, SR], I32)
        wrow = sb("wrow", [P, 4, 2, SR])

        ps = ctx.enter_context(nc.psum_tensor("ps", [P, 8, 512], F32))

        def bank(i):
            return ps[:, i, :]

        def bank16(i):
            return ps[:, i, :].bitcast(F16)

        def const(name):
            a, b = CF[name]
            return cfs[:, a:b]

        identh, upper, ones16 = chs[:, 0:P], chs[:, P:2 * P], chs[:, 2 * P:3 * P]
        ident = const("ident")

        names = """x_in0 x_in1 xr_in x2_out small_in wq_in wo_in const_in st_in0 st_in1 pads_in pad_out zero_out
            setup split_high split_low we_scaled we_high we_low
            ln1_stats ln1_mv ln1_var rstd1 xn_ready xh_ready xl_ready t1_done xT_ready kp_done qp_done vp_done
            sig_k dec_ready sig_q v_ready scan_prep scan_done mid_done rmid_done e_done q_done qt_ready re_done kt_ready
            a_done at_ready kt_done kts_ready kv_done sm_ready ot_done ots_ready sq_ready ss_done ssv_ready rms_ready
            y_done x2_ready ln2_stats ln2_mv ln2_var rstd2 xn2_ready rowhi_ready rowlo_ready x2t_done x2T_ready lg_done
            route_a wsig_ready rk_done route_b tok_ready disp0 disp1 plan_done
            xg_in0 xg_in1 xg_in2 xg_in3 tx_done xtc_ready g1_done sv_ready h_ready g2_done y_ready meta_ready w_ready added held""".split()
        S = {n: sem(n) for n in names}
        x_in, disp, st_in = ([S[f"{n}{i}"] for i in range(2)] for n in ("x_in", "disp", "st_in"))
        xg_in = [S[f"xg_in{i}"] for i in range(4)]

        rows32 = rows[:].bitcast(F32)
        rows_i = rows[:].bitcast(I32)
        wq_stage = qt[:].rearrange("p a h l -> p (a h l)")[:, 0:3 * KD * D]

        def flat(t):
            names = " ".join("abcde"[:len(t.shape) - 1])
            return t[:].rearrange(f"p {names} -> p ({names})") if len(t.shape) > 2 else t[:]

        def row_buffer(t, i):
            return t[:, i.slot // 2, i.slot % 2 * SR:(i.slot % 2 + 1) * SR]

        def xTm(i):
            return flat(xT)[:, i.par * 4 * RT:(i.par + 1) * 4 * RT].rearrange("p (q t) -> p q t", t=RT)

        def silu_of(i):
            return flat((kk, qq)[i.par]).rearrange("p (q t) -> p q t", t=RT)

        def value_of(i):
            return flat((ff, at)[i.par]).rearrange("p (q t) -> p q t", t=RT)

        def hhl(i):
            return flat((ots, xn2)[i.par]).bitcast(F16).rearrange("p (a q t) -> p a q t", a=2, t=RT)

        def y_of(i):
            return flat(x2T)[:, i.par * SR * D:(i.par + 1) * SR * D].rearrange("p (s d) -> p s d", d=D)

        block = ctx.enter_context(nc.Block())

        x_v = x.rearrange("(s p) d -> p s d", p=P)
        out_v = out.rearrange("(s p) d -> p s d", p=P)

        def wait(eng, name, value):
            if isinstance(value, int) and value <= 0:
                return
            eng.wait_ge(S[name] if isinstance(name, str) else name, value)

        def wait_apart(eng, *waits):
            for name, v in waits:
                wait(eng, name, v)
                if not isinstance(v, int):
                    eng.sem_inc(S["held"], 1)

        def pipelined(eng, first, last, one, unroll=2):
            assert (last - first + 1) % unroll == 0
            with eng.Fori(0, (last - first + 1) // unroll) as j:
                for u in range(unroll):
                    one(j, first + u)

        def stages(c):
            return [0 <= q < NSEQ for q in (c + 3, c + 2, c + 1, c, c - 1)]

        def iterations(eng, one, first=-3):
            for c in range(first, 1):
                one(0, c)
            pipelined(eng, 1, 4, one)
            for c in range(5, NSEQ + 1):
                one(0, c)

        @block.sync
        def _(sp):
            sp.dma_start(cfs[:], cf).then_inc(S["const_in"], 16)
            sp.dma_start(xs[:, 0], x_v[:, 0:C]).then_inc(x_in[0], 16)
            sp.dma_start(chs[:], ch).then_inc(S["const_in"], 16)
            sp.dma_start(qt[:].rearrange("p a h l -> p (a h l)")[:, 0:3 * KD * D], wqkv).then_inc(S["wq_in"], 16)
            sp.dma_start(xs[:, 1], x_v[:, C:2 * C]).then_inc(x_in[1], 16)
            sp.dma_start(wos[:], wo).then_inc(S["wo_in"], 16)
            sp.dma_start(nws[:], norm_w).then_inc(S["wo_in"], 16)
            sp.dma_start(gws[:], gate_w).then_inc(S["small_in"], 16)
            sp.dma_start(b1s[:], b1).then_inc(S["small_in"], 16)
            for p in range(2):
                sp.dma_start(vv[p:p + 1].rearrange("p a c d -> p (a c d)"), b2).then_inc(S["small_in"], 16)
            sp.dma_start(pads[:], pad).then_inc(S["pads_in"], 16)
            sp.dma_start(xr[:], x_v[:, 0:C]).then_inc(S["xr_in"], 16)
            sp.wait_ge(S["pads_in"], 16)
            sp.dma_start(rows_dram[SPARE:SPARE + RT, :].rearrange("(s p) n -> p s n", p=P), pads[:]).then_inc(S["pad_out"], 16)
            sp.wait_ge(S["setup"], 1)
            sp.dma_start(out_v[:, T // P:T // P + SR, :], resets[:, 0:SR * D].rearrange("p (s d) -> p s d", d=D)).then_inc(S["zero_out"], 16)

            def weights_in(m, slot):
                wait_apart(sp, ("we_low", m - 1))
                sp.dma_start(wst[:, slot], we[:, bass.ds(m * WCH, WCH)]).then_inc(st_in[slot], 16)

            weights_in(0, 0)
            weights_in(1, 1)

            def one(j, c):
                b = Seq(j, c)

                def weights(q):
                    if 0 <= c and c * CPS + q + 2 < NCH:
                        weights_in(b.n * CPS + 2 + q, (CPS * c + q) % 2)

                weights(0)
                if c + 3 < NSEQ:
                    a = Seq(j, c + 3)
                    wait_apart(sp, ("xl_ready", b.upto(1, 2)),
                                   ("ss_done", b.upto(1)))
                    sp.dma_start(xs[:, a.par], x_v[:, bass.ds(a.n * C, C)]).then_inc(x_in[a.par], 16)
                if 0 <= c:
                    wait_apart(sp, ("x2_ready", b.upto(C)))
                    sp.dma_start(out_v[:, bass.ds(b.n * C, C)], xr[:]).then_inc(S["x2_out"], 16)
                weights(1)
                if 0 <= c < NSEQ - 1:
                    wait_apart(sp, ("x2_out", b.upto(16)), ("xn2_ready", b.upto(C)))
                    a = Seq(j, c + 1)
                    sp.dma_start(xr[:], x_v[:, bass.ds(a.n * C, C)]).then_inc(S["xr_in"], 16)
                weights(2)

            one(0, -1)
            one(0, 0)
            pipelined(sp, 1, 4, one)
            for c in range(5, NSEQ):
                one(0, c)
            sp.wait_ge(S["plan_done"], 1)
            for e in range(E):
                row = sp.value_load(plani[0:1, 2, e:e + 1], min_val=0, max_val=SPARE - RT)
                sp.dma_start(rows_dram[bass.ds(row, RT), :].rearrange("(s p) n -> p s n", p=P), pads[:]).then_inc(S["pad_out"], 16)
            sp.wait_ge(S["plan_done"], PLAN)
            sp.wait_ge(S["pad_out"], 16 * (E + 1))
            for i in range(2):
                sp.wait_ge(disp[i], 16 * 2 * C * NSEQ // 2)

            def tile_in(j, c):
                i = Tile(j, c)
                wait_apart(sp, ("tx_done", i.upto(1, -3)),
                               ("meta_ready", i.upto(2, -6)))
                row = sp.value_load(roff[0:1, bass.ds(i.n, 1)], min_val=0, max_val=SPARE)
                sp.dma_start(row_buffer(rows_i, i), rows_dram[bass.ds(row, RT), :].rearrange("(s p) n -> p s n", p=P)).then_inc(xg_in[i.slot], 16)

            for c in range(7):
                tile_in(0, c)
            pipelined(sp, 7, NT - 1, tile_in, 4)
            sp.wait_ge(S["x2_out"], 16 * NSEQ)
            sp.wait_ge(S["zero_out"], 16)
            sp.wait_ge(S["added"], 32 * NT)


        @block.tensor
        def _(pe):
            def chunk(c):
                return slice(c * P, (c + 1) * P)

            def transposed_x(b, part):
                wait(pe, "xT_ready", b.upto(2, 0))
                wait(pe, "x2_ready", b.upto(C, -C))
                wait(pe, ("xh_ready", "xl_ready")[part], b.upto(1))
                for k in range(KD):
                    for c in range(C):
                        mm = pe.transpose(bank16(part)[:, k * L + c * P:k * L + (c + 1) * P],
                                          xhl[:, part, c, k * P:(k + 1) * P], identh)
                mm.then_inc(S["t1_done"], 1)

            def three(o, lhs, rhs):
                terms = [(k, a, c) for k in range(KD) for a, c in ((0, 0), (0, 1), (1, 0))]
                for n, (k, a, c) in enumerate(terms):
                    mm = pe.matmul(o, lhs(a, k), rhs(c, k), start=n == 0, stop=n == len(terms) - 1)
                return mm

            def project_heads(b, which, name):
                for h in range(NH):
                    if which == 1:
                        wait(pe, "v_ready", b.upto(2, h - 1))
                        if h == 0:
                            wait(pe, "xT_ready", b.upto(2))
                    else:
                        wait(pe, "sig_k", b.upto(2 * NH, 2 * h + 2))
                    three(bank(2 + h), lambda a, k: wp[:, a, which, k, h * P:(h + 1) * P],
                          lambda a, k: xT[:, a, k, :]).then_inc(S[name], 1)

            def project_v(b):
                for pair in range(2):
                    wait(pe, "q_done", b.upto(NH, pair + 1))
                    for c in range(2 * pair, 2 * pair + 2):
                        mm = three(bank(2 + pair)[:, c % 2 * D:(c % 2 + 1) * D],
                                   lambda a, k: xT[:, a, k, chunk(c)], lambda a, k: wp[:, a, 2, k, :])
                    mm.then_inc(S["vp_done"], 1)

            def scores(b):
                wait(pe, "qt_ready", b.upto(1))
                wait(pe, "ssv_ready", b.upto(1, 0))
                wait(pe, "route_b", b.upto(ROUTE_B, 2 - 2 * ROUTE_B))
                for h in range(NH):
                    wait(pe, "kt_ready", b.upto(NH, h + 1))
                    for c in range(C):
                        mm = pe.matmul(bank(4 + h)[:, chunk(c)], kk[:, h, chunk(c)], qt[:, b.par, h, chunk(c)],
                                       start=True, stop=True)
                    mm.then_inc(S["a_done"], 1)

            def keys(b):
                for h in range(NH):
                    wait(pe, "sq_ready", b.upto(NH, h + 1 - NH))
                    for c in range(C - 1):
                        mm = pe.transpose(bank(6 + h)[:, chunk(c)], kk[:, h, chunk(c)], ident)
                    mm.then_inc(S["kt_done"], 1)

            def states(b):
                wait(pe, "at_ready", b.upto(2 * NH))
                wait(pe, "kts_ready", b.upto(NH))
                wait(pe, "v_ready", b.upto(2))
                for h in range(NH):
                    for c in range(C - 1):
                        mm = pe.matmul(bank(4 + h)[:, chunk(c)], kTs[:, h, c, :], vv[:, b.par, c, h * P:(h + 1) * P],
                                       start=True, stop=True)
                mm.then_inc(S["kv_done"], 1)

            def outputs(b):
                wait(pe, "sm_ready", b.upto(5))
                for h in range(NH):
                    for c in range(C):
                        mm = pe.matmul(bank(6 + h)[:, chunk(c)], vv[:, b.par, c, h * P:(h + 1) * P], at[:, h, c, :],
                                       start=True, stop=c == 0)
                        if c:
                            mm = pe.matmul(bank(6 + h)[:, chunk(c)], sm[:, c - 1, h, :], qt[:, b.par, h, chunk(c)],
                                           start=False, stop=True)
                    mm.then_inc(S["ot_done"], 1)

            def squares(b):
                wait(pe, "sq_ready", b.upto(NH))
                for c in range(C):
                    for h in range(NH):
                        mm = pe.matmul(bank(4)[:, c:c + 1], xs[:, 1 - b.par].rearrange("p c d -> p (c d)")[:, h * L + c * P:h * L + (c + 1) * P],
                                       const("ones")[:, 0:1], start=h == 0, stop=h == NH - 1)
                mm.then_inc(S["ss_done"], 1)

            def mixed(b, last):
                if not last:
                    wait(pe, "xT_ready", b.upto(2, 4))
                wait(pe, "x2T_ready", b.upto(KD, 0))
                for c in range(C):
                    for h in range(NH):
                        mm = pe.matmul(bank(c // 2)[:, c % 2 * D:(c % 2 + 1) * D], ots[:, h, chunk(c)], wos[:, h, :],
                                       start=h == 0, stop=h == NH - 1)
                    if c % 2:
                        mm.then_inc(S["y_done"], 1)

            def transposed_x2(b, last):
                wait(pe, "xn2_ready", b.upto(C))
                if not last:
                    wait(pe, "xT_ready", b.upto(2, 6))
                for k in range(KD):
                    for c in range(C):
                        mm = pe.transpose(bank(k)[:, chunk(c)], xn2[:, c, k * P:(k + 1) * P], ident)
                    mm.then_inc(S["x2t_done"], 1)

            def gates(b, last=False):
                wait(pe, "x2T_ready", b.upto(KD))
                if not last:
                    wait(pe, "sm_ready", b.upto(5, 10))
                for c in range(C):
                    for k in range(KD):
                        mm = pe.matmul(bank(5)[:, c * E:(c + 1) * E], x2T[:, k, chunk(c)], gws[:, k, :],
                                       start=k == 0, stop=k == KD - 1)
                mm.then_inc(S["lg_done"], 1)

            def ranks(b):
                wait(pe, "route_a", b.upto(ROUTE_A))
                for c in range(C):
                    for d in range(c + 1):
                        mm = pe.matmul(bank(5)[:, 64 + c * E:64 + (c + 1) * E], upper if d == c else ones16, msel[:, d, :],
                                       start=d == 0, stop=d == c)
                for d in range(C):
                    mm = pe.matmul(bank(5)[:, 128:128 + E], ones16, msel[:, d, :], start=d == 0, stop=d == C - 1)
                mm.then_inc(S["rk_done"], 1)

            def one(j, c):
                t, n, p, m, r = stages(c)
                a2, a1, a, b, z = (Seq(j, c + 3 - q) for q in range(5))
                last = m and not p
                if p:
                    project_heads(a, 1, "kp_done")
                if r:
                    transposed_x2(z, last=not p)
                if p:
                    project_heads(a, 0, "qp_done")
                if r and p:
                    gates(z, last=not m)
                if m:
                    outputs(b)
                if r and not p:
                    gates(z, last=not m)
                if r and not last:
                    ranks(z)
                if m:
                    squares(b)
                    mixed(b, last=not p)
                if r and last:
                    ranks(z)
                if p:
                    project_v(a)
                if p:
                    scores(a)
                    keys(a)
                if n:
                    transposed_x(a1, 0)
                    transposed_x(a1, 1)
                if p:
                    states(a)

            pe.wait_ge(S["const_in"], 32)
            pe.wait_ge(S["small_in"], 64)
            pe.wait_ge(S["split_low"], 1)
            one(0, -2)
            one(0, -1)
            pe.wait_ge(S["setup"], SETUP)
            iterations(pe, one, 0)

            def tile_transposed(i):
                wait(pe, xg_in[i.slot], i.turn * 16 + 16)
                wait(pe, "xtc_ready", i.upto(1, -1))
                for part in range(2):
                    for k in range(KD):
                        for s in range(SR):
                            mm = pe.transpose(bank16(4 + i.par)[:, (2 * part + k) * RT + s * P:(2 * part + k) * RT + (s + 1) * P],
                                              row_buffer(rows, i)[:, s, part * D + k * P:part * D + (k + 1) * P], identh)
                mm.then_inc(S["tx_done"], 1)

            def up(i, e):
                pe.wait_ge(S["xtc_ready"], i.upto(1))
                for j in range(FJ):
                    wait(pe, "sv_ready", i.upto(2 * FJ, 2 * j + 2 - 2 * FJ))
                    for g in range(2):
                        terms = [(k, a, c) for k in range(KD) for a, c in ((0, 0), (0, 1), (1, 0))]
                        for n, (k, a, c) in enumerate(terms):
                            lhs = wes[:, a, bass.ds(e * (KD * 2 * FF) + (k * 2 * FF + g * FF + j * P), P)]
                            mm = pe.matmul(bank(j)[:, g * RT:(g + 1) * RT], lhs, xTm(i)[:, 2 * c + k, :],
                                           start=n == 0, stop=n == len(terms) - 1)
                    mm.then_inc(S["g1_done"], 1)

            def down(i, e):
                pe.wait_ge(S["h_ready"], i.upto(4))
                wait(pe, "y_ready", i.upto(SR, -SR))
                for s in range(SR):
                    o = bank(6 + i.par)[:, s * D:(s + 1) * D]
                    pe.matmul(o, ones2[0:2, :], b2s[0:2, bass.ds(e * D, D)], start=True, stop=False)
                    for j in range(FJ):
                        for a, c in ((0, 0), (1, 0), (0, 1)):
                            rhs = wes[:, c, bass.ds(e * (FJ * D) + (W1COLS + j * D), D)]
                            mm = pe.matmul(o, hhl(i)[:, a, j, s * P:(s + 1) * P], rhs, start=False, stop=j == FJ - 1 and (a, c) == (0, 1))
                mm.then_inc(S["g2_done"], 1)

            def tile(j, c, t=True, u=True, d=True):
                i = Tile(j, c)
                if t:
                    tile_transposed(Tile(j, c + 1))
                if u:
                    up(i, pe.value_load(etab[0:1, bass.ds(i.n, 1)], min_val=0, max_val=E - 1))
                if d:
                    z = Tile(j, c - 1)
                    down(z, pe.value_load(etab[0:1, bass.ds(z.n, 1)], min_val=0, max_val=E - 1))

            tile(0, -1, u=False, d=False)
            tile(0, 0, d=False)
            for c in range(1, 5):
                tile(0, c)
            pipelined(pe, 5, NT - 3, tile, 4)
            tile(0, NT - 2)
            tile(0, NT - 1, t=False)
            tile(0, NT, t=False, u=False)

        @block.scalar
        def _(act):
            act.wait_ge(S["wq_in"], 16)
            act.activation(wq_stage, wq_stage, ACT.Copy, scale=SW).then_inc(S["split_high"], 1)
            act.wait_ge(S["split_high"], 1)
            act.activation(wp[:, 0].rearrange("p q k d -> p (q k d)"), wq_stage, ACT.Copy).then_inc(S["split_high"], 1)

            def split_weights(b, q, slot):
                m = b.n * CPS + q
                act.wait_ge(st_in[slot], (CPS * b.j + (CPS * b.c + q) // 2) * 16 + 16)
                act.activation(wst[:, slot], wst[:, slot], ACT.Copy, scale=SW).then_inc(S["we_scaled"], 1)
                act.wait_ge(S["we_scaled"], m + 1)
                act.activation(wes[:, 0, bass.ds(m * WCH, WCH)], wst[:, slot], ACT.Copy).then_inc(S["we_high"], 1)

            def high(a):
                wait(act, "xn_ready", a.upto(C))
                wait(act, "t1_done", a.upto(2, -1))
                act.activation(xhl[:, 0], xs[:, a.par], ACT.Copy).then_inc(S["xh_ready"], 1)

            def transposed(a, part):
                wait(act, "t1_done", a.upto(2, part + 1))
                wait(act, "vp_done", a.upto(2, 0))
                act.activation(xT[:, part], bank16(part).rearrange("p (k t) -> p k t", t=L), ACT.Copy)\
                    .then_inc(S["xT_ready"], 1)

            def one(j, c):
                t, n, p, m, r = stages(c)
                a2, a1, a, b, z = (Seq(j, c + 3 - q) for q in range(5))
                slot = lambda q: (CPS * c + q) % 2
                if p:
                    for h in range(NH):
                        act.wait_ge(S["kp_done"], a.upto(NH, h + 1))
                        if h == 0:
                            wait(act, "kt_ready", a.upto(NH, 0))
                        act.activation(ff[:, h * L:(h + 1) * L], bank(2 + h), ACT.Sigmoid, scale=1 / (SX * SW)).then_inc(S["sig_k"], 1)
                        wait(act, "kt_done", a.upto(NH, 0))
                        act.activation(kk[:, h], bank(2 + h), ACT.Sigmoid, scale=-1 / (SX * SW)).then_inc(S["sig_k"], 1)
                if p:
                    act.wait_ge(S["sig_k"], a.upto(2 * NH))
                    act.activation(ff[:], ff[:], ACT.Sigmoid).then_inc(S["dec_ready"], 1)
                if r:
                    for k in range(KD):
                        act.wait_ge(S["x2t_done"], z.upto(KD, k + 1))
                        wait(act, "lg_done", z.upto(1, 0))
                        act.activation(x2T[:, k], bank(k), ACT.Copy).then_inc(S["x2T_ready"], 1)
                    wait(act, disp[z.par], z.half * (2 * C * 16))
                    act.activation(rows[:, z.par, :, 0:D], xn2[:], ACT.Copy).then_inc(S["rowhi_ready"], 1)
                if p:
                    for h in range(NH):
                        act.wait_ge(S["qp_done"], a.upto(NH, h + 1))
                        wait(act, "qt_ready", a.upto(1, 0))
                        act.activation(qq[:, h], bank(2 + h), ACT.Sigmoid, scale=1 / (SX * SW)).then_inc(S["sig_q"], 1)
                if m:
                    if p:
                        split_weights(b, 0, slot(0))
                    sq = xs[:, 1 - b.par].rearrange("p c d -> p (c d)")
                    for h in range(NH):
                        act.wait_ge(S["ot_done"], b.upto(NH, h + 1))
                        wait(act, "y_done", b.upto(2, 0))
                        act.activation(ots[:, h], bank(6 + h), ACT.Copy).then_inc(S["ots_ready"], 1)
                        act.activation(sq[:, h * L:(h + 1) * L], bank(6 + h), ACT.Square).then_inc(S["sq_ready"], 1)
                if r:
                    act.wait_ge(S["route_a"], z.upto(ROUTE_A))
                    for i, sign in enumerate((1, -1)):
                        act.activation(wsig[:, i], gap[:], ACT.Sigmoid, scale=sign / SX).then_inc(S["wsig_ready"], 1)
                if m:
                    for q in range(1 if p else 0, CPS):
                        split_weights(b, q, slot(q))
                if n:
                    wait(act, "xn_ready", a1.upto(C))
                    wait(act, "t1_done", a1.upto(2, -1))
                    act.activation(xhl[:, 0], xs[:, a1.par], ACT.Copy).then_inc(S["xh_ready"], 1)
                if p:
                    for pair in range(2):
                        act.wait_ge(S["vp_done"], a.upto(2, pair + 1))
                        act.activation(vv[:, a.par, 2 * pair:2 * pair + 2].rearrange("p c d -> p (c d)"), bank(2 + pair), ACT.Copy,
                                       scale=1 / (SX * SW)).then_inc(S["v_ready"], 1)
                if p:
                    for h in range(NH):
                        wait(act, "kt_done", a.upto(NH, h + 1))
                        act.activation(kTs[:, h], bank(6 + h)[:, 0:(C - 1) * P].rearrange("p (c t) -> p c t", t=P),
                                       ACT.Copy).then_inc(S["kts_ready"], 1)
                if n:
                    transposed(a1, 0)
                    transposed(a1, 1)

            for c in range(-2, 3):
                one(0, c)
            pipelined(act, 3, 4, one)
            for c in range(5, NSEQ + 1):
                one(0, c)

            act.wait_ge(S["setup"], SETUP)

            def tile(j, c, t=True, u=True):
                i = Tile(j, c)
                if t:
                    a = Tile(j, c + 1)
                    act.wait_ge(S["tx_done"], a.upto(1))
                    wait(act, "g1_done", a.upto(FJ, -FJ))
                    act.activation(xTm(a), bank16(4 + a.par).rearrange("p (q t) -> p q t", t=RT), ACT.Copy).then_inc(S["xtc_ready"], 1)
                if u:
                    e = act.value_load(etab[0:1, bass.ds(i.n, 1)], min_val=0, max_val=E - 1)
                    wait(act, "h_ready", i.upto(4, -4))
                    for q in range(FJ):
                        act.wait_ge(S["g1_done"], i.upto(FJ, q + 1))
                        act.activation(silu_of(i)[:, q, :], bank(q)[:, 0:RT], ACT.Silu, bias=b1s[:, bass.ds(e * 2 * FJ + q, 1)],
                                       scale=ALPHA / (SX * SW)).then_inc(S["sv_ready"], 1)
                        act.activation(value_of(i)[:, q, :], bank(q)[:, RT:2 * RT], ACT.Identity,
                                       bias=b1s[:, bass.ds(e * 2 * FJ + (FJ + q), 1)],
                                       scale=SH / (ALPHA * SX * SW)).then_inc(S["sv_ready"], 1)

            tile(0, -1, u=False)
            tile(0, 0)
            for c in range(1, 5):
                tile(0, c)
            pipelined(act, 5, NT - 3, tile, 4)
            tile(0, NT - 2)
            tile(0, NT - 1, t=False)

        @block.vector
        def _(dve):
            def row_stats(b, src, st_, mv_, stats_sem, mv_sem):
                for c in range(C):
                    dve.bn_stats(st_[:, c, :], src[:, c, :]).then_inc(S[stats_sem], 1)
                wait_apart(dve, (S[stats_sem], b.upto(C)))
                for c in range(C):
                    dve.bn_aggr(mv_[:, c, :], st_[:, c, :]).then_inc(S[mv_sem], 1)

            def stats1(a):
                dve.wait_ge(x_in[a.par], a.upto_half(16))
                row_stats(a, xs[:, a.par], st, mv1, "ln1_stats", "ln1_mv")

            def normalise1(a):
                dve.wait_ge(S["rstd1"], a.upto(1))
                for c in range(C):
                    dve.tensor_scalar(xs[:, a.par, c], xs[:, a.par, c], mv1[:, c, 0:1], rs1[:, c:c + 1], ALU.subtract, ALU.mult)\
                        .then_inc(S["xn_ready"], 1)

            def decays(a):
                d = ff[:].rearrange("p (g s t) -> p g s t", s=2, t=HALF)
                starts = ff[:].rearrange("p (g t) -> p g t", t=HALF)[:, :, 0]
                dve.wait_ge(S["dec_ready"], a.upto(1))
                dve.tensor_copy(resets[:].rearrange("p (g t) -> p g t", t=HALF)[:, :, 0], starts).then_inc(S["scan_prep"], 1)
                dve.wait_ge(S["scan_prep"], a.upto(2, 1))
                dve.memset(starts, 0.0).then_inc(S["scan_prep"], 1)
                dve.wait_ge(S["scan_prep"], a.upto(2))
                dve.tensor_tensor_scan(ff[:], ff[:], resets[:], 0.0, ALU.mult, ALU.add).then_inc(S["scan_done"], 1)
                dve.wait_ge(S["scan_done"], a.upto(1))
                dve.tensor_copy(dmid[:], d[:, :, 0, HALF - 1]).then_inc(S["mid_done"], 1)
                dve.tensor_copy(dend[:], d[:, :, 1, HALF - 1]).then_inc(S["mid_done"], 1)
                dve.wait_ge(S["mid_done"], a.upto(3, 2))
                dve.reciprocal(rmid[:], dmid[:]).then_inc(S["rmid_done"], 1)
                dv, mv = dend[:].rearrange("p (h c) -> p h c", c=C), dmid[:].rearrange("p (h c) -> p h c", c=C)
                dve.tensor_tensor(gg[:], dv[:, :, 0:C - 1], mv[:, :, 1:C], ALU.mult).then_inc(S["mid_done"], 1)
                dve.wait_ge(S["rmid_done"], a.upto(1))
                dve.tensor_tensor(d[:, :, 0, :], d[:, :, 0, :], rmid[:].unsqueeze(2).broadcast_to((P, NH * C, HALF)), ALU.mult)\
                    .then_inc(S["e_done"], 1)

            def queries(a):
                for h in range(NH):
                    dve.wait_ge(S["sig_q"], a.upto(NH, h + 1))
                    dve.scalar_tensor_tensor(out=qq[:, h], in0=bank(2 + h), scalar=1 / (SX * SW), in1=qq[:, h],
                                             op0=ALU.mult, op1=ALU.mult).then_inc(S["q_done"], 1)
                dve.wait_ge(S["q_done"], a.upto(NH))
                dve.wait_ge(S["e_done"], a.upto(1))
                dve.tensor_tensor(flat(qt)[:, a.par * NH * L:(a.par + 1) * NH * L], flat(qq), ff[:], ALU.mult).then_inc(S["qt_ready"], 1)

            def inverse_decays(a, h):
                f = ff[:, h * L:(h + 1) * L]
                dve.reciprocal(f, f).then_inc(S["re_done"], 1)

            def masks(b):
                wait(dve, "ot_done", b.upto(NH, 0))
                m = const("mask")
                for h in range(NH):
                    dve.wait_ge(S["a_done"], b.upto(NH, h + 1))
                    sc = bank(4 + h).rearrange("p (c t) -> p c t", t=P)
                    dve.tensor_tensor(at[0:HALF, h], sc[0:HALF], m[0:HALF].unsqueeze(1).broadcast_to((HALF, C, P)), ALU.mult)\
                        .then_inc(S["at_ready"], 1)
                    dve.tensor_tensor(at[HALF:P, h, :, HALF:P], sc[HALF:P, :, HALF:P],
                                      m[HALF:P, HALF:P].unsqueeze(1).broadcast_to((HALF, C, HALF)), ALU.mult).then_inc(S["at_ready"], 1)

            def states(b):
                dve.wait_ge(S["kv_done"], b.upto(1))
                kv = ps[:, 4:4 + NH, :]
                g = lambda c: gg[:, :, c:c + 1].broadcast_to((P, NH, P))
                dve.tensor_tensor(sm[:, 0], kv[:, :, 0:P], g(0), ALU.mult).then_inc(S["sm_ready"], 1)
                for c in (1, 2):
                    dve.wait_ge(S["sm_ready"], b.upto(5, 2 * c - 1))
                    dve.tensor_tensor(smt[:], kv[:, :, c * P:(c + 1) * P], sm[:, c - 1], ALU.add).then_inc(S["sm_ready"], 1)
                    dve.wait_ge(S["sm_ready"], b.upto(5, 2 * c))
                    dve.tensor_tensor(sm[:, c], smt[:], g(c), ALU.mult).then_inc(S["sm_ready"], 1)

            def chain(name, z, per):
                k = [0]

                def step(ins, hold=True):
                    ins.then_inc(S[name], 1)
                    k[0] += 1
                    if hold:
                        dve.wait_ge(S[name], z.upto(per, k[0]) if z else k[0])
                    return k[0]
                return step, k

            def route_a(z):
                wait_apart(dve, ("lg_done", z.upto(1)))
                step, k = chain("route_a", z, ROUTE_A)
                logits = bank(5)[:, 0:C * E].rearrange("p (c e) -> p c e", e=E)
                for c in range(C):
                    step(dve.max(lmax[:, c, :], logits[:, c, :]), hold=False)
                wait_apart(dve, ("route_a", z.upto(ROUTE_A, C)))
                for c in range(C):
                    step(dve.max_index(lidx[:, c, :], lmax[:, c, :], logits[:, c, :]), hold=c == C - 1)
                step(dve.tensor_copy(chosen[:].rearrange("p i c -> p c i"), lidx[:, :, 0:2]))
                experts = const("eidx").unsqueeze(1).unsqueeze(1).broadcast_to((P, 2, C, E))
                step(dve.tensor_tensor(onehot[:], experts, chosen[:].unsqueeze(3).broadcast_to((P, 2, C, E)), ALU.is_equal))
                step(dve.tensor_tensor(gap[:], lmax[:, :, 0], lmax[:, :, 1], ALU.subtract), hold=False)
                step(dve.tensor_tensor(msel[:], onehot[:, 0], onehot[:, 1], ALU.add), hold=False)
                assert k[0] == ROUTE_A

            def route_b(z):
                dve.wait_ge(S["rowhi_ready"], z.upto(1))
                dve.wait_ge(S["rk_done"], z.upto(1))
                step, k = chain("route_b", z, ROUTE_B)
                rank = bank(5)[:, 64:64 + C * E].rearrange("p (c e) -> p c e", e=E)
                step(dve.tensor_tensor(places[:], rank, cnt[:].unsqueeze(1).broadcast_to((P, C, E)), ALU.add))
                step(dve.tensor_tensor(cnt[:], cnt[:], bank(5)[:, 128:128 + E], ALU.add), hold=False)
                step(dve.tensor_tensor(picked[:], onehot[:], places[:].unsqueeze(1).broadcast_to((P, 2, C, E)), ALU.mult))
                step(dve.tensor_reduce(place[:], picked[:], AX, ALU.add))
                step(dve.tensor_copy(dest[:, z.par], place[:]), hold=False)
                dve.wait_ge(S["wsig_ready"], z.upto(2))
                words = rows32[:, z.par]
                step(dve.tensor_copy(words[:, :, D + 3], chosen[:, 0]), hold=False)
                step(dve.tensor_scalar(words[:, :, D + 1], wsig[:, 1], 1 / (SH * SW), None, ALU.mult))
                step(dve.scalar_tensor_tensor(out=words[:, :, D + 2], in0=wsig[:, 0], scalar=1 / (SH * SW), in1=words[:, :, D + 1],
                                              op0=ALU.mult, op1=ALU.subtract), hold=False)
                assert k[0] == ROUTE_B

            def residual(b):
                dve.wait_ge(S["rms_ready"], b.upto(1))
                dve.wait_ge(S["xr_in"], b.upto(16))
                for c in range(C):
                    if c % 2 == 0:
                        dve.wait_ge(S["y_done"], b.upto(2, c // 2 + 1))
                    dve.scalar_tensor_tensor(out=xr[:, c], in0=bank(c // 2)[:, c % 2 * D:(c % 2 + 1) * D], scalar=rms[:, c:c + 1],
                                             in1=xr[:, c], op0=ALU.mult, op1=ALU.add).then_inc(S["x2_ready"], 1)

            def normalise2(b):
                dve.wait_ge(S["rstd2"], b.upto(1))
                wait(dve, "x2t_done", b.upto(KD, 0))
                wait(dve, "rowlo_ready", b.upto(1, 0))
                for c in range(C):
                    dve.tensor_scalar(xn2[:, c], xr[:, c], mv2[:, c, 0:1], rs2[:, c:c + 1], ALU.subtract, ALU.mult)\
                        .then_inc(S["xn2_ready"], 1)

            def one(j, c):
                t, n, p, m, r = stages(c)
                a2, a1, a, b, z = (Seq(j, c + 3 - q) for q in range(5))
                last = m and not p
                if p:
                    decays(a)
                if r:
                    route_a(z)
                if p:
                    queries(a)
                if r and not last:
                    route_b(z)
                if p:
                    dve.wait_ge(S["qt_ready"], a.upto(1))
                    inverse_decays(a, 0)
                if m:
                    dve.wait_ge(S["ss_done"], b.upto(1))
                    dve.tensor_scalar(ssv[:], bank(4)[:, 0:C], 1 / D, EPS_RMS, ALU.mult, ALU.add).then_inc(S["ssv_ready"], 1)
                if p:
                    inverse_decays(a, 1)
                if n:
                    normalise1(a1)
                if m:
                    residual(b)
                if p:
                    masks(a)
                if m:
                    dve.wait_ge(S["x2_ready"], b.upto(C))
                    row_stats(b, xr, st2, mv2, "ln2_stats", "ln2_mv")
                if t:
                    stats1(a2)
                if r and last:
                    route_b(z)
                if m:
                    normalise2(b)
                if p:
                    states(a)

            step, k = chain("setup", None, 0)
            step(dve.memset(resets[:], 0.0), hold=False)
            step(dve.memset(at[HALF:P, :, :, 0:HALF], 0.0), hold=False)
            step(dve.memset(ones2[:], SW), hold=False)
            one(0, -3)
            one(0, -2)
            dve.wait_ge(S["split_high"], 2)
            dve.tensor_tensor(wp[:, 1].rearrange("p q k d -> p (q k d)"), wq_stage, wp[:, 0].rearrange("p q k d -> p (q k d)"),
                              ALU.subtract).then_inc(S["split_low"], 1)
            dve.wait_ge(S["const_in"], 32)
            dve.wait_ge(S["small_in"], 64)
            dve.wait_ge(S["wo_in"], 32)
            step(dve.tensor_copy(cnt[:], const("base")), hold=False)
            for h in range(NH):
                step(dve.tensor_scalar(wos[:, h], wos[:, h], nws[:, h:h + 1], None, ALU.mult), hold=False)
            b1v = b1s[:].rearrange("p (e g j) -> p e g j", g=2, j=FJ)
            step(dve.tensor_scalar(b1v[:, :, 0], b1v[:, :, 0], ALPHA, None, ALU.mult), hold=False)
            step(dve.tensor_scalar(b1v[:, :, 1], b1v[:, :, 1], 1.0, SH / ALPHA, ALU.add, ALU.mult), hold=False)
            b2v = flat(vv)[0:2, :]
            step(dve.tensor_scalar(b2v, b2v, SH, None, ALU.mult))
            step(dve.tensor_copy(b2s[:], b2v))
            step(dve.scalar_tensor_tensor(out=b2s[:], in0=b2s[:], scalar=cfs[0:2, CF["low"][0]:CF["low"][1]], in1=b2v,
                                          op0=ALU.mult, op1=ALU.add), hold=False)
            dve.wait_ge(S["zero_out"], 16)
            step(dve.memset(resets[:, 0:1], 0.0))
            assert k[0] == SETUP

            iterations(dve, one, -1)

            step, k = chain("plan_done", None, 0)
            ptile = flat(x2T)[:, 0:3 * NT * E].rearrange("p (a t e) -> p a t e", a=3, e=E)
            cols = lambda v: v.unsqueeze(1).broadcast_to((P, NT, E))
            tiles = lambda v: v.unsqueeze(2).broadcast_to((P, NT, E))
            step(dve.tensor_copy(plani[:, 2], cnt[:]))
            step(dve.tensor_tensor(plan[:, 0], cnt[:], const("base"), ALU.subtract))
            step(dve.tensor_scalar(plani[:, 0], plan[:, 0], float(RT - 1), None, ALU.add))
            step(dve.tensor_scalar(plani[:, 1], plani[:, 0], RT.bit_length() - 1, None, ALU.logical_shift_right))
            step(dve.tensor_copy(plan[:, 0], plani[:, 1]))
            step(dve.tensor_tensor_scan(plan[:, 1], const("ones"), plan[:, 0], 0.0, ALU.mult, ALU.add))
            step(dve.tensor_tensor(plan[:, 2], plan[:, 1], plan[:, 0], ALU.subtract))
            step(dve.scalar_tensor_tensor(out=plan[:, 3], in0=plan[:, 2], scalar=-float(RT), in1=const("base"),
                                          op0=ALU.mult, op1=ALU.add))
            step(dve.tensor_tensor(ptile[:, 0], cols(plan[:, 1]), tiles(const("tile")), ALU.is_le))
            step(dve.tensor_reduce(pt[:, 0], ptile[:, 0], AX, ALU.add))
            step(dve.tensor_tensor(ptile[:, 1], tiles(pt[:, 0]), cols(const("eidx")), ALU.is_equal))
            step(dve.tensor_tensor(ptile[:, 2], ptile[:, 1], cols(plan[:, 3]), ALU.mult))
            step(dve.tensor_reduce(pt[:, 1], ptile[:, 2], AX, ALU.add))
            step(dve.tensor_scalar(pt[:, 2], pt[:, 0], float(E), None, ALU.is_lt))
            step(dve.tensor_tensor(pt[:, 3], pt[:, 2], const("tile_row"), ALU.mult))
            step(dve.tensor_tensor(pt[:, 1], pt[:, 1], pt[:, 3], ALU.add))
            step(dve.tensor_scalar(roff[:], pt[:, 1], float(SPARE), None, ALU.add), hold=False)
            step(dve.tensor_scalar(etab[:], pt[:, 0], float(E - 1), None, ALU.min), hold=False)
            assert k[0] == PLAN

            def tile(j, c, u=True, d=True):
                i, z = Tile(j, c), Tile(j, c - 1)
                if u:
                    h = flat(xs)[:, 0:FJ * RT]
                    v, g = (t(i).rearrange("p q t -> p (q t)") for t in (value_of, silu_of))
                    hi, lo = (hhl(i)[:, n].rearrange("p q t -> p (q t)") for n in range(2))
                    dve.wait_ge(S["sv_ready"], i.upto(2 * FJ))
                    dve.tensor_scalar(v, v, (LIMIT + 1) * SH / ALPHA, (1 - LIMIT) * SH / ALPHA, ALU.min, ALU.max).then_inc(S["h_ready"], 1)
                    dve.wait_ge(S["h_ready"], i.upto(4, 1))
                    dve.scalar_tensor_tensor(out=h, in0=g, scalar=SILU_MAX, in1=v, op0=ALU.min, op1=ALU.mult).then_inc(S["h_ready"], 1)
                    dve.wait_ge(S["h_ready"], i.upto(4, 2))
                    wait(dve, "g2_done", i.upto(1, -1))
                    dve.tensor_copy(hi, h).then_inc(S["h_ready"], 1)
                    dve.wait_ge(S["h_ready"], i.upto(4, 3))
                    dve.tensor_tensor(lo, h, hi, ALU.subtract).then_inc(S["h_ready"], 1)
                if d:
                    dve.wait_ge(S["g2_done"], z.upto(1))
                    dve.wait_ge(S["w_ready"], z.upto(WSTEPS))
                    wait(dve, "added", z.upto(32, -32))
                    for s in range(SR):
                        dve.tensor_scalar(y_of(z)[:, s], bank(6 + z.par)[:, s * D:(s + 1) * D], wrow[:, z.slot, 1, s:s + 1], None,
                                          ALU.mult).then_inc(S["y_ready"], 1)

            tile(0, 0, d=False)
            for c in range(1, 5):
                tile(0, c)
            pipelined(dve, 5, NT - 3, tile, 4)
            tile(0, NT - 2)
            tile(0, NT - 1)
            tile(0, NT, u=False)

        @block.gpsimd
        def _(pool):
            pool.wait_ge(S["const_in"], 32)

            def rstd(b, mv_, var_sem, out_, out_sem, mv_sem):
                wait_apart(pool, (S[mv_sem], b.upto(C)))
                pool.tensor_scalar(pw[:, 0], mv_[:, :, 1], EPS_LN, None, ALU.add).then_inc(S[var_sem], 1)
                pool.wait_ge(S[var_sem], b.upto(2, 1))
                pool.tensor_tensor(pw[:, 1], pw[:, 0], const("half"), ALU.pow).then_inc(S[var_sem], 1)
                wait_apart(pool, (S[var_sem], b.upto(2)))
                pool.tensor_scalar(out_[:], pw[:, 1], SX, None, ALU.mult).then_inc(S[out_sem], 1)

            def one(j, c):
                t, n, p, m, r = stages(c)
                a2, a1, a, b, z = (Seq(j, c + 3 - q) for q in range(5))
                if r:
                    wait_apart(pool, ("rowhi_ready", z.upto(1)))
                    pool.tensor_tensor(rows[:, z.par, :, D:2 * D], xn2[:], rows[:, z.par, :, 0:D], ALU.subtract).then_inc(S["rowlo_ready"], 1)
                    at_ = CF["tok"][0]
                    pool.tensor_copy(rows_i[:, z.par, :, D], cfs[:].bitcast(I32)[:, bass.ds(z.n * C + at_, C)]).then_inc(S["tok_ready"], 1)

                def dispatch(c_):
                    for i in range(2):
                        pool.indirect_dma_start(rows_dram, bass.IndirectOffsetOnAxis(ap=dest[:, z.par, i, c_:c_ + 1], axis=0),
                                                rows_i[:, z.par, c_, :], None).then_inc(disp[z.par], 16)

                def divided_keys(h):
                    pool.wait_ge(S["re_done"], a.upto(NH, h + 1))
                    pool.tensor_tensor(kk[:, h], kk[:, h], ff[:, h * L:(h + 1) * L], ALU.mult).then_inc(S["kt_ready"], 1)

                def low_parts(q):
                    m, slot = b.n * CPS + q, (CPS * c + q) % 2
                    pool.wait_ge(S["we_high"], m + 1)
                    pool.tensor_tensor(wes[:, 1, bass.ds(m * WCH, WCH)], wst[:, slot], wes[:, 0, bass.ds(m * WCH, WCH)],
                                       ALU.subtract).then_inc(S["we_low"], 1)

                def root_mean_square():
                    pool.wait_ge(S["ssv_ready"], b.upto(1))
                    pool.tensor_tensor(rms[:], ssv[:], const("half"), ALU.pow).then_inc(S["rms_ready"], 1)

                def first_dispatch():
                    wait_apart(pool, ("route_b", z.upto(ROUTE_B)), ("rowlo_ready", z.upto(1)), ("tok_ready", z.upto(1)))
                    dispatch(0)
                    dispatch(1)

                last = m and not p
                if m and not last:
                    low_parts(0)
                if r and not last:
                    first_dispatch()
                if p:
                    divided_keys(0)
                if m:
                    root_mean_square()
                if p:
                    divided_keys(1)
                if n:
                    wait_apart(pool, ("xh_ready", a1.upto(1)), ("t1_done", a1.upto(2, 0)))
                    pool.tensor_tensor(xhl[:, 1], xs[:, a1.par], xhl[:, 0], ALU.subtract).then_inc(S["xl_ready"], 1)
                if last:
                    low_parts(0)
                if m:
                    low_parts(1)
                    rstd(b, mv2, "ln2_var", rs2, "rstd2", "ln2_mv")
                if t:
                    rstd(a2, mv1, "ln1_var", rs1, "rstd1", "ln1_mv")
                if r and last:
                    first_dispatch()
                if r:
                    dispatch(2)
                if m:
                    low_parts(2)
                if r:
                    dispatch(3)

            iterations(pool, one)

            pool.wait_ge(S["plan_done"], PLAN)
            pool.wait_ge(S["x2_out"], 16 * NSEQ)
            pool.wait_ge(S["zero_out"], 16)

            def tile(j, c, u=True, d=True):
                i, z = Tile(j, c), Tile(j, c - 1)
                if u:
                    wait_apart(pool, (xg_in[i.slot], i.turn * 16 + 16),
                                     ("added", i.upto(32, -96)))
                    m = meta[:, i.slot]
                    pool.tensor_copy(token[:, i.slot], row_buffer(rows_i, i)[:, :, D]).then_inc(S["meta_ready"], 1)
                    pool.tensor_copy(m, row_buffer(rows32, i)[:, :, D + 1:D + 4]).then_inc(S["meta_ready"], 1)
                    pool.wait_ge(S["meta_ready"], i.upto(2))
                    ef = pt[:, 0, bass.ds(i.n, 1)].broadcast_to((P, SR))
                    same, w = wrow[:, i.slot, 0], wrow[:, i.slot, 1]
                    pool.tensor_tensor(same, m[:, :, 2], ef, ALU.subtract).then_inc(S["w_ready"], 1)
                    wait_apart(pool, ("w_ready", i.upto(WSTEPS, 1)))
                    pool.tensor_scalar(same, same, 0.0, None, ALU.is_equal).then_inc(S["w_ready"], 1)
                    pool.wait_ge(S["w_ready"], i.upto(WSTEPS, 2))
                    pool.tensor_tensor(w, same, m[:, :, 1], ALU.mult).then_inc(S["w_ready"], 1)
                    pool.wait_ge(S["w_ready"], i.upto(WSTEPS, 3))
                    pool.tensor_tensor(w, w, m[:, :, 0], ALU.add).then_inc(S["w_ready"], 1)
                if d:
                    wait_apart(pool, ("y_ready", z.upto(SR)),
                                     ("added", z.upto(32, 0)))
                    for s in range(SR):
                        pool.indirect_dma_start(out, bass.IndirectOffsetOnAxis(ap=token[:, z.slot, s:s + 1], axis=0),
                                                y_of(z)[:, s], None, compute_op=ALU.add).then_inc(S["added"], 16)

            tile(0, 0, d=False)
            for c in range(1, 5):
                tile(0, c)
            pipelined(pool, 5, NT - 3, tile, 4)
            tile(0, NT - 2)
            tile(0, NT - 1)
            tile(0, NT, u=False)


def constants():
    import numpy as np

    cf = np.zeros((P, CFN), np.float32)
    p = np.arange(P)

    def put(name, v):
        a, b = CF[name]
        cf[:, a:b] = v

    put("ident", np.eye(P))
    put("mask", p[:, None] <= p[None, :])
    put("base", np.arange(E) * REGION)
    put("eidx", np.arange(E))
    put("tile", np.arange(NT))
    put("tile_row", np.arange(NT) * RT - SPARE)
    put("half", -0.5)
    put("ones", 1.0)
    put("low", -1.0 * (p[:, None] == 1))
    a, b = CF["tok"]
    cf[:, a:b].view(np.int32)[:] = np.arange(T // P)[None, :] * P + p[:, None]
    ch = np.concatenate([np.eye(P), p[:, None] < p[None, :], np.ones((P, P))], 1).astype(np.float16)
    words = np.zeros((P, SR, WORDS), np.int32)
    words[:, :, D] = T + np.arange(SR)[None, :] * P + p[:, None]
    words[:, :, D + 3] = np.float32(-1.0).view(np.int32)
    return cf, ch, words


def kernel(L0_attn_x, L0_attn_Wq, L0_attn_Wk, L0_attn_Wv, L0_attn_Wo, L0_attn_norm_w, L0_ffn_gate_w,
           L0_ffn_dense_1_w, L0_ffn_dense_1_b, L0_ffn_dense_2_w, L0_ffn_dense_2_b):
    import numpy as np
    import concourse.bacc as bacc
    from concourse.bass_utils import run_bass_kernel_spmd

    def halves(w):
        return np.asarray(w).T.reshape(KD, P, D).transpose(1, 0, 2)

    x = np.ascontiguousarray(np.asarray(L0_attn_x).reshape(T, D))
    wqkv = np.stack([halves(w) for w in (L0_attn_Wq, L0_attn_Wk, L0_attn_Wv)], 1).reshape(P, 3 * KD * D)
    wo = np.ascontiguousarray(halves(L0_attn_Wo))
    norm_w = np.ascontiguousarray(np.asarray(L0_attn_norm_w).reshape(NH, P).T)
    gate_w = np.ascontiguousarray(np.asarray(L0_ffn_gate_w).reshape(KD, P, E).transpose(1, 0, 2))
    w1 = np.asarray(L0_ffn_dense_1_w).reshape(E, FF, 2, KD, P).transpose(4, 0, 3, 2, 1).reshape(P, W1COLS)
    w2 = np.asarray(L0_ffn_dense_2_w).reshape(E, D, FJ, P).transpose(3, 0, 2, 1).reshape(P, W2COLS)
    we = np.concatenate([w1, w2], 1)
    b1 = np.ascontiguousarray(np.asarray(L0_ffn_dense_1_b).reshape(E, FJ, P, 2).transpose(2, 0, 3, 1).reshape(P, E * 2 * FJ))
    b2 = np.ascontiguousarray(np.asarray(L0_ffn_dense_2_b).reshape(1, E * D))
    cf, ch, pad = constants()
    arrays = dict(x=x, wqkv=wqkv, wo=wo, norm_w=norm_w, gate_w=gate_w, we=we, b1=b1, b2=b2, cf=cf, ch=ch, pad=pad)

    nc = bacc.Bacc("TRN2", target_bir_lowering=False, num_devices=1)
    args = [nc.dram_tensor(n, a.shape, mybir.dt.from_np(a.dtype), kind="ExternalInput").ap() for n, a in arrays.items()]
    args.append(nc.dram_tensor("out", (T + RT, D), F32, kind="ExternalOutput").ap())
    build_kernel(nc, *args)
    got = run_bass_kernel_spmd(nc, [arrays], core_ids=[0]).results[0]["out"]
    return got[0:T].reshape(NSEQ, L, D)
```
